# Optimizing a Trainium2 kernel written in Bass

```python
import numpy as np
import jax
import jax.numpy as jnp

def _softmax(x, axis=-1):
    return jax.nn.softmax(x, axis=axis)

def _gelu(x):
    return jax.nn.gelu(x, approximate=True)

def _silu(x):
    return jax.nn.silu(x)

def _sigmoid(x):
    return jax.nn.sigmoid(x)

def _layernorm(x, axis=-1, eps=1e-05):
    m = jnp.mean(x, axis=axis, keepdims=True)
    v = jnp.var(x, axis=axis, keepdims=True)
    return (x - m) / jnp.sqrt(v + eps)

def _scatter_add(tgt, idx, src, axis=0):
    return tgt.at[idx].add(src)

def _segment_sum(src, seg, n):
    return jax.ops.segment_sum(src, seg, n)
kernel_name = 'mk_prb_d1_jaxref_r4_607e33'

def setup_inputs(seed: int=0):
    np.random.seed(seed)
    _w = jnp.asarray

    def _L0_attn_setup():
        import jax, jax.numpy as jnp
        import numpy as np
        EMBED_DIM = 256
        NUM_HEADS = 16
        HEAD_DIM = EMBED_DIM // NUM_HEADS
        SCALING = HEAD_DIM ** (-0.5)
        key = jax.random.key(seed)
        k1, k2, k3, k4, k5 = jax.random.split(key, 5)
        B, S, E, H = (2, 512, EMBED_DIM, NUM_HEADS)
        x = jax.random.normal(k1, (B, S, E), dtype=jnp.float32)
        W_A = jax.random.normal(k2, (H, E), dtype=jnp.float32) * E ** (-0.5)
        W_V = jax.random.normal(k3, (E, E), dtype=jnp.float32) * E ** (-0.5)
        W_O = jax.random.normal(k4, (E, E), dtype=jnp.float32) * E ** (-0.5)
        b_O = jax.random.normal(k5, (E,), dtype=jnp.float32) * 0.01
        return {'x': x, 'W_A': W_A, 'W_V': W_V, 'W_O': W_O, 'b_O': b_O}
    _L0_attn_in = _L0_attn_setup()

    def _L0_ffn_setup():
        import jax, jax.numpy as jnp
        import numpy as np
        B, S, D, E, K = (4, 512, 256, 8, 2)
        H = 4 * D
        key = jax.random.key(seed)
        k0, k1, k2, k3 = jax.random.split(key, 4)
        x = jax.random.normal(k0, (B, S, D), dtype=jnp.float32)
        router_w = jax.random.normal(k1, (E, D), dtype=jnp.float32) * 0.02
        w1 = jax.random.normal(k2, (E, H, D), dtype=jnp.float32) * 0.02
        w2 = jax.random.normal(k3, (E, D, H), dtype=jnp.float32) * 0.02
        return {'x': x, 'router_w': router_w, 'w1': w1, 'w2': w2}
    _L0_ffn_in = _L0_ffn_setup()
    _d = {'L0_attn_x': _L0_attn_in['x'], 'L0_attn_W_A': _L0_attn_in['W_A'], 'L0_attn_W_V': _L0_attn_in['W_V'], 'L0_attn_W_O': _L0_attn_in['W_O'], 'L0_attn_b_O': _L0_attn_in['b_O'], 'L0_ffn_router_w': _L0_ffn_in['router_w'], 'L0_ffn_w1': _L0_ffn_in['w1'], 'L0_ffn_w2': _L0_ffn_in['w2']}
    _x0 = _d['L0_attn_x']
    _d['L0_attn_x'] = jax.random.normal(jax.random.fold_in(jax.random.key(seed), 1), (4, 1024, 256), dtype=_x0.dtype)
    del _x0
    return _d

def reference(L0_attn_x, L0_attn_W_A, L0_attn_W_V, L0_attn_W_O, L0_attn_b_O, L0_ffn_router_w, L0_ffn_w1, L0_ffn_w2):

    def _L0_attn_ref(x, W_A, W_V, W_O, b_O):
        import jax, jax.numpy as jnp
        import numpy as np
        EMBED_DIM = 256
        NUM_HEADS = 16
        HEAD_DIM = EMBED_DIM // NUM_HEADS
        SCALING = HEAD_DIM ** (-0.5)
        B, S, E = x.shape
        H, D = (NUM_HEADS, HEAD_DIM)
        z = jnp.einsum('bse,he->bsh', x, W_A) * SCALING
        z = jax.nn.softmax(z, axis=1)
        zp = jnp.transpose(z, (0, 2, 1))
        i = jnp.arange(S)[:, None]
        j = jnp.arange(S)[None, :]
        idx = (i - j) % S
        tril = (j <= i).astype(x.dtype)
        roll = zp[:, :, idx] * tril
        v = jnp.einsum('bse,fe->bsf', x, W_V).reshape(B, S, H, D)
        out = jnp.einsum('bhij,bjhd->bihd', roll, v).reshape(B, S, E)
        return jnp.einsum('bse,fe->bsf', out, W_O) + b_O

    def _L0_ffn_ref(x, router_w, w1, w2):
        import jax, jax.numpy as jnp
        import numpy as np
        B, S, D, E, K = (4, 512, 256, 8, 2)
        H = 4 * D
        b, s, d = x.shape
        e = router_w.shape[0]
        logits = jnp.einsum('bsd,ed->bse', x, router_w)
        probs = jax.nn.softmax(logits, axis=-1)
        topk_vals, topk_idx = jax.lax.top_k(probs, K)
        x_flat = x.reshape(b * s, d)
        vals = topk_vals.reshape(b * s, K)
        idx = topk_idx.reshape(b * s, K)
        out = jnp.zeros_like(x_flat)
        for eid in range(e):
            w = jnp.sum(jnp.where(idx == eid, vals, jnp.zeros((), x.dtype)), axis=-1)
            h = jax.nn.gelu(x_flat @ w1[eid].T, approximate=False)
            y = h @ w2[eid].T
            out = out + w[:, None] * y
        return out.reshape(b, s, d)
    x = L0_attn_x
    xn = _layernorm(x, axis=-1)
    x = x + _L0_attn_ref(xn, L0_attn_W_A, L0_attn_W_V, L0_attn_W_O, L0_attn_b_O) + _L0_ffn_ref(xn, L0_ffn_router_w, L0_ffn_w1, L0_ffn_w2)
    return x

_drawn_inputs = setup_inputs


def setup_inputs(seed=0):
    import zlib

    import numpy as np

    out = dict(_drawn_inputs(seed))
    spreads = {}
    factors = {'L0_attn_W_A': 2.862, 'L0_attn_b_O': 5.825}
    for name, (base, spread) in spreads.items():
        noise = np.random.default_rng([zlib.crc32(name.encode()), seed]).standard_normal(out[name].shape)
        drawn = base * np.exp(spread * noise) if base else spread * noise
        out[name] = jnp.asarray(drawn.astype(out[name].dtype))
    for name, factor in factors.items():
        out[name] = (out[name] * factor).astype(out[name].dtype)
    return out
```

```python
from contextlib import ExitStack

import concourse.bass as bass
from concourse import mybir

F32 = mybir.dt.float32
BF16 = mybir.dt.bfloat16
I32 = mybir.dt.int32
U32 = mybir.dt.uint32
ALU = mybir.AluOpType
ACT = mybir.ActivationFunctionType
AX = mybir.AxisListType

P = 128
B, S, D = 4, 1024, 256
NH, HD = 16, 16
NE, H = 8, 1024
TOK = B * S
NT = TOK // P
NJ = S // P
GT = 4
KD = D // P
KH = H // P
NP = NE + NH + D
TS = 256
NTILE = (2 * TOK) // TS + NE - 1
NCOL = NTILE * TS // P
ROW = D + NE
PADROWS = 2 * P
NZ = S + P
HG = 4
NG = NH // HG
EARLY, MID, LATE = 6, 4, 6
CHUNK = 2048
XS = 3
SCALE = float(HD) ** -0.5
EPS = 1e-5

C_ID, C_TP1, C_P, C_EW, C_S, C_PAD = 0, 128, 192, 193, 201, 201 + NTILE * (NE - 1)
C_F = C_PAD + NCOL
C_UT, C_ONE, C_IR, C_IA = 0, 128, 256, 384
C_B = C_IA + NCOL

CHUNKS = ([(1, e) for e in range(0, 6)] + [(2, e) for e in range(4, 8)]
          + [(1, 6), (1, 7)] + [(2, e) for e in range(0, 4)])


def build(nc, x, routerT, waT, wvT, woT, b_o, w1T, w2T, const_f, const_b, zeros, out):
    x_t = x.rearrange("(g t p) d -> g p t d", p=P, t=GT)
    x_b = x.rearrange("(b t p) d -> b p t d", p=P, t=NJ)
    out_b = out[0:TOK, :].rearrange("(b t p) d -> b p t d", p=P, t=NJ)
    w1_v = w1T.rearrange("e (k p) h -> e p k h", p=P)
    w2_v = w2T.rearrange("e (c p) d -> e p c d", p=P)

    with ExitStack() as ctx:
        xn_dram = nc.dram_tensor("xn_table", [TOK + PADROWS, ROW], F32).ap()
        z_dram = nc.dram_tensor("z_padded", [B, NH, 2, NZ], BF16).ap()
        xn_rows = xn_dram[0:TOK, :].rearrange("(g t p) d -> g p t d", p=P, t=GT)
        xn_w8 = xn_dram[0:TOK, :].rearrange("(t p) d -> p t d", p=P)

        cursor = [16512]

        def at(name, shape, dt, offset):
            return nc.alloc_sbuf_tensor_at(name, shape, dt, offset=offset)

        def sb(name, shape, dt, zone=None):
            size = 4 if dt in (F32, I32, U32) else 2
            for n in shape[1:]:
                size *= n
            c = cursor if zone is None else zone
            t = at(name, shape, dt, c[0])
            c[0] += (size + 31) // 32 * 32
            return t

        w1_at = cursor[0]
        w1s = sb("w1s", [P, NE, 2, KD, H], BF16)
        w2_at = cursor[0]
        w2s = sb("w2s", [P, NE, KH, 2 * D], BF16)
        stage = sb("w_stage", [P, 2, CHUNK], F32)

        vs = at("v_split", [P, 2, B, NH, NJ, HD], BF16, w2_at)
        zone = [w2_at + 4 * KH * 2 * D * 2]
        xin = sb("x_in", [P, 2, GT, D], F32, zone)
        xnb = sb("xn_buf", [P, 2, GT, D], F32, zone)
        ez = sb("z_exp", [NH, S], F32, zone)
        zhl = sb("z_split", [NH, 2, NZ], BF16, zone)
        xnT = sb("xnT", [P, 2, KD, P], F32, zone)
        wcat = sb("w_cat", [P, KD, NP], F32, zone)
        assert zone[0] <= w2_at + NE * KH * 2 * D * 2
        zone = [w1_at + 6 * 2 * KD * H * 2]
        prob = sb("prob", [P, NT, NE], F32, zone)
        t8 = sb("route_t8", [P, NT, NE], F32, zone)
        oh1 = sb("onehot1", [P, NT, NE], F32, zone)
        oh2 = sb("onehot2", [P, NT, NE], F32, zone)
        rank = sb("rank", [P, NT, NE], F32, zone)
        maskb = sb("mask_bf", [P, NT, NE], BF16, zone)
        ohr = sb("onehot_r", [P, 16, P], BF16, zone)
        oha = sb("onehot_a", [P, 16, 2, NCOL], BF16, zone)
        c32 = sb("cols32", [P, 4, NT], F32, zone)
        posf = sb("pos_f", [P, 2, NT], F32, zone)
        posi = sb("pos_i", [P, 2, NT], I32, zone)
        assert zone[0] <= w2_at

        ffn_at = cursor[0]
        tz = sb("toeplitz", [P, 2, HG, 2, S], BF16)
        ao = sb("attn_out", [P, NJ, D], F32)
        xr = sb("resid", [P, NJ, D], F32)
        zone = [ffn_at]
        xs = sb("x_sorted", [P, XS, 2, ROW], F32, zone)
        xT = sb("xT_split", [P, 2, KD, TS], BF16, zone)
        act = sb("gelu", [P, 4, 2 * TS], F32, zone)
        gh = sb("gelu_hi", [P, KH, TS], BF16, zone)
        gl = sb("gelu_lo", [P, KH, TS], BF16, zone)
        yt = sb("y_lo", [P, 2, D], F32, zone)
        y = sb("y", [P, 2, D], F32, zone)
        assert zone[0] <= cursor[0]

        wo = sb("w_o", [P, KD, D], F32)
        aoT = sb("attn_outT", [P, 2, KD, P], F32)
        bo = sb("b_o", [P, D], F32)
        cf = sb("const_f", [P, C_F], F32)
        cb = sb("const_b", [P, C_B], BF16)
        lg = sb("logits", [P, NJ, NE + NH], F32)
        lg8 = sb("router_logits", [P, NT, NE], F32)
        st = sb("stats", [P, GT, 6], F32)
        mv = sb("mean_var", [P, 2, GT, 2], F32)
        std = sb("std", [P, 2, GT], F32)
        rstd = sb("rstd", [P, 2, GT], F32)
        zst = sb("z_stats", [NH, 4], F32)
        eps = sb("eps", [P, 1], F32)
        colA = sb("place_col", [P, 2 * NT], F32)
        colR = sb("place_row", [P, 2 * NT], F32)
        e8 = sb("per_expert", [P, 6, NE], F32)
        e8i = sb("per_expert_i", [P, 2, NE], I32)
        msum = sb("mask_sum", [P, NE], BF16)
        ge9 = sb("tile_ge", [P, NTILE, NE + 1], F32)
        teoh = sb("tile_onehot", [P, NTILE, NE], F32)
        tef = sb("tile_expert_f", [P, NTILE], F32)
        tei = sb("tile_expert", [P, NTILE], I32)
        idf = sb("list_f", [P, 2, NCOL], F32)
        idt = sb("list", [P, NCOL], U32)
        idxs = sb("gather_index", [P, XS, 2], U32)
        g8 = sb("gate8", [P, 2, NE], F32)
        gate = sb("gate", [P, 2], F32)
        held = sb("held", [P, 2], F32)
        assert cursor[0] <= nc.sbuf_usable_end, cursor[0]

        bank = [ctx.enter_context(nc.psum_tensor(f"bank{i}", [P, 512], F32)) for i in range(4)]
        psz = ctx.enter_context(nc.psum_tensor("bank45", [P, 2, 512], F32))
        bank6 = ctx.enter_context(nc.psum_tensor("bank6", [P, 512], F32))
        bank7 = ctx.enter_context(nc.psum_tensor("bank7", [P, 512], F32))
        ps_t, ps_p = bank[0:2], bank[2:4]
        ps_c = [psz[:, 0, :], psz[:, 1, :]]
        ps_rank = bank6[:, 0:NT * NE]
        ps_cnt = bank7[:, 256:256 + NE]
        ps_list = bank7[:, 0:2 * NCOL]

        ident = cf[:, C_ID:C_ID + P]

        names = ("const_in w_in x_in0 x_in1 stats_done aggr_done std_done rstd_done xn_done xn_out0 xn_out1 "
                 "tp_done xnT_done proj_done lg_done lg8_done vhi_done post_done ztp_done zmax_done zneg_done "
                 "zexp_done zrec_done zn_done zhi_done zsplit_done z_out zpad_done stage_in0 stage_in1 whi_done "
                 "wlo_done wlate_done T_in0 T_in1 conv_done aoevac_done aotp_done aoT_done wo_done res_done "
                 "xr_in xrb_done out_init route route_exp rsub_done mask_done cnt_done w8_out pads_out onehots "
                 "listmm_done list_done g_in0 g_in1 g_in2 idx_done xtp_done xhi_done xlo_done g1_done gelu_done "
                 "glo_done g2_done ylo_done y_done g8_done gate_done acc_out eps_done held_done")
        sem = {n: ctx.enter_context(nc.semaphore(n)) for n in names.split()}
        (const_in, w_in, x_in0, x_in1, stats_done, aggr_done, std_done, rstd_done, xn_done, xn_out0, xn_out1,
         tp_done, xnT_done, proj_done, lg_done, lg8_done, vhi_done, post_done, ztp_done, zmax_done, zneg_done,
         zexp_done, zrec_done, zn_done, zhi_done, zsplit_done, z_out, zpad_done, stage_in0, stage_in1, whi_done,
         wlo_done, wlate_done, T_in0, T_in1, conv_done, aoevac_done, aotp_done, aoT_done, wo_done, res_done,
         xr_in, xrb_done, out_init, route, route_exp, rsub_done, mask_done, cnt_done, w8_out, pads_out, onehots,
         listmm_done, list_done, g_in0, g_in1, g_in2, idx_done, xtp_done, xhi_done, xlo_done, g1_done, gelu_done,
         glo_done, g2_done, ylo_done, y_done, g8_done, gate_done, acc_out, eps_done, held_done) = sem.values()
        x_in, xn_out, stage_in, T_in, g_in = ((x_in0, x_in1), (xn_out0, xn_out1), (stage_in0, stage_in1),
                                              (T_in0, T_in1), (g_in0, g_in1, g_in2))
        CONSTS = 3
        WEIGHTS = 5

        def w_split(c):
            m, e = CHUNKS[c]
            if m == 1:
                return w1s[:, e, 0], w1s[:, e, 1], stage[:, c % 2, :].rearrange("p (k h) -> p k h", k=KD)
            return (w2s[:, e, :, 0:D], w2s[:, e, :, D:2 * D],
                    stage[:, c % 2, :].rearrange("p (c d) -> p c d", d=D))

        block = ctx.enter_context(nc.Block())

        @block.sync
        def _(sp):
            sp.dma_start(cf[:, :], const_f).then_inc(const_in, 16)
            sp.dma_start(xin[:, 0], x_t[0]).then_inc(x_in0, 16)
            sp.dma_start(xin[:, 1], x_t[1]).then_inc(x_in1, 16)
            sp.dma_start(wcat[:, :, 0:NE], routerT.rearrange("(k p) n -> p k n", p=P)).then_inc(w_in, 16)
            sp.dma_start(wcat[:, :, NE:NE + NH], waT.rearrange("(k p) n -> p k n", p=P)).then_inc(w_in, 16)
            sp.dma_start(wcat[:, :, NE + NH:NP], wvT.rearrange("(k p) n -> p k n", p=P)).then_inc(w_in, 16)
            sp.dma_start(wo[:, :, :], woT.rearrange("(k p) n -> p k n", p=P)).then_inc(w_in, 16)
            sp.dma_start(bo[:, :], b_o.partition_broadcast(P)).then_inc(w_in, 16)
            sp.dma_start(cb[:, :], const_b).then_inc(const_in, 16)
            sp.dma_start(xn_dram[TOK:TOK + PADROWS, :], zeros).then_inc(pads_out, 16)
            sp.dma_start(out[TOK:TOK + PADROWS, :], zeros[:, 0:D]).then_inc(out_init, 16)
            sp.dma_start(xr[:, :, :], x_b[0]).then_inc(xr_in, 16)

            def toeplitz(n):
                b, g = n // NG, n % NG
                if n % NG == 0:
                    sp.wait_ge(z_out, 16 * (b + 1))
                if n >= 2:
                    sp.wait_ge(conv_done, n - 1)
                src = bass.AP(z_dram.tensor, (b * NH + g * HG) * 2 * NZ,
                              [[1, P], [NZ, HG * 2], [1, S]])
                sp.dma_start(tz[:, n % 2].rearrange("p h l s -> p (h l) s"), src).then_inc(T_in[n % 2], 16)

            for b in range(B):
                for r in range(2):
                    n = 2 * b + r
                    sp.wait_ge(xn_done, GT * (n + 1))
                    sp.dma_start(xn_rows[n, :, :, 0:D], xnb[:, r]).then_inc(xn_out[r], 16)
                    if n + 2 < 2 * B:
                        sp.dma_start(xin[:, r], x_t[n + 2]).then_inc(x_in[r], 16)
                    if b == 1:
                        toeplitz(r)
                sp.wait_ge(zsplit_done, b + 1)
                sp.dma_start(z_dram[b], zhl[:, :, :]).then_inc(z_out, 16)
            sp.wait_ge(mask_done, 1)
            sp.dma_start(xn_w8[:, :, D:ROW], t8[:, :, :]).then_inc(w8_out, 16)
            for n in range(2, B * NG):
                toeplitz(n)
                if n % NG == 1 and n > NG:
                    b = n // NG - 1
                    sp.wait_ge(res_done, NJ * (b + 1))
                    sp.dma_start(out_b[b], xr[:, :, :]).then_inc(out_init, 16)
                    sp.wait_ge(out_init, 16 * (b + 2))
                    sp.dma_start(xr[:, :, :], x_b[b + 1]).then_inc(xr_in, 16)
            sp.wait_ge(res_done, NJ * B)
            sp.dma_start(out_b[B - 1], xr[:, :, :]).then_inc(out_init, 16)
            sp.wait_ge(out_init, 16 * (B + 1))

        @block.gpsimd
        def _(pool):
            def load_chunk(c):
                if c >= 2:
                    if c - 2 < EARLY + MID:
                        pool.wait_ge(wlo_done, c - 1)
                    else:
                        pool.wait_ge(wlate_done, c - 1 - EARLY - MID)
                m, e = CHUNKS[c]
                _, _, s = w_split(c)
                nc.gpsimd.dma_start(s, (w1_v if m == 1 else w2_v)[e]).then_inc(stage_in[c % 2], 16)

            def split_lo(c):
                hi, lo, s = w_split(c)
                pool.wait_ge(stage_in[c % 2], 16 * (c // 2 + 1))
                pool.wait_ge(whi_done, c + 1)
                nc.gpsimd.tensor_tensor(lo, s, hi, ALU.subtract).then_inc(wlo_done, 1)

            nc.gpsimd.memset(held[:, :], 0.0).then_inc(held_done, 1)
            pool.wait_ge(held_done, 1)
            nc.gpsimd.memset(zhl[:, :, S:NZ], 0.0).then_inc(zpad_done, 1)
            load_chunk(0)
            load_chunk(1)
            for c in range(EARLY + MID):
                split_lo(c)
                load_chunk(c + 2)
                if c == EARLY - 1:
                    pool.wait_ge(w_in, 16 * WEIGHTS)
                    pool.wait_ge(xr_in, 16)
                    nc.gpsimd.tensor_tensor(xr[:, :, :], xr[:, :, :],
                                            bo[:, :].unsqueeze(1).to_broadcast([P, NJ, D]),
                                            ALU.add).then_inc(xrb_done, 1)
            for b in range(1, B):
                pool.wait_ge(xr_in, 16 * (b + 1))
                nc.gpsimd.tensor_tensor(xr[:, :, :], xr[:, :, :],
                                        bo[:, :].unsqueeze(1).to_broadcast([P, NJ, D]),
                                        ALU.add).then_inc(xrb_done, 1)
            for c in range(EARLY + MID + 2, len(CHUNKS)):
                load_chunk(c)

            def hold(k):
                pool.wait_ge(held_done, k + 1)
                nc.gpsimd.tensor_tensor(held[:, 1:2], held[:, 0:1], held[:, 0:1], ALU.add).then_inc(held_done, 1)

            def gather(n, s):
                nc.gpsimd.tensor_copy(idxs[:, s, :], idt[:, bass.ds(2 * n, 2)]).then_inc(idx_done, 1)
                pool.wait_ge(idx_done, n + 1)
                hold(n if isinstance(n, int) and n < XS else 3 * n - 4)
                for m in range(2):
                    nc.gpsimd.indirect_dma_start(
                        out=xs[:, s, m, :], out_offset=None, in_=xn_dram[:, :],
                        in_offset=bass.IndirectOffsetOnAxis(ap=idxs[:, s, m:m + 1], axis=0),
                    ).then_inc(g_in[s], 16)

            def scatter(n, s, ended=0):
                for m in range(2):
                    pool.wait_ge(y_done, 2 * n + m + 1)
                    if not (isinstance(n, int) and n == 0 and m == 0):
                        pool.wait_ge(acc_out, 16 * (2 * n + m))
                    hold(XS + 3 * n + m - ended)
                    nc.gpsimd.indirect_dma_start(
                        out=out[:, :], out_offset=bass.IndirectOffsetOnAxis(ap=idxs[:, s, m:m + 1], axis=0),
                        in_=y[:, m, :], in_offset=None, compute_op=ALU.add,
                    ).then_inc(acc_out, 16)

            pool.wait_ge(list_done, 1)
            pool.wait_ge(xn_out0, 16 * B)
            pool.wait_ge(xn_out1, 16 * B)
            pool.wait_ge(w8_out, 16)
            pool.wait_ge(pads_out, 16)
            pool.wait_ge(conv_done, B * NG)
            for n in range(XS):
                gather(n, n)
            pool.wait_ge(out_init, 16 * (B + 1))
            scatter(0, 0)
            pool.wait_ge(acc_out, 32)
            gather(XS, 0)
            for n in range(1, XS):
                scatter(n, n)
                pool.wait_ge(acc_out, 32 * n + 32)
                gather(n + XS, n)
            with pool.Fori(1, NTILE // XS - 1) as i:
                for s in range(XS):
                    n = XS * i + s
                    scatter(n, s)
                    pool.wait_ge(acc_out, 32 * n + 32)
                    gather(n + XS, s)
            for n in range(NTILE - XS, NTILE):
                scatter(n, n % XS, n - NTILE + XS)
            pool.wait_ge(acc_out, 32 * NTILE)

        @block.scalar
        def _(a):
            def std_group(n, r):
                a.wait_ge(aggr_done, GT * (n + 1))
                nc.scalar.activation(std[:, r], mv[:, r, :, 1], ACT.Sqrt, bias=eps[:, :]).then_inc(std_done, 1)

            def whi(c, q=None):
                hi, _, s = w_split(c)
                if q is None or q == 0:
                    a.wait_ge(stage_in[c % 2], 16 * (c // 2 + 1))
                if q is None:
                    nc.scalar.activation(hi, s, ACT.Copy).then_inc(whi_done, 1)
                    return
                w = H // 2
                ins = nc.scalar.activation(hi[:, q // 2, w * (q % 2):w * (q % 2 + 1)],
                                           s[:, q // 2, w * (q % 2):w * (q % 2 + 1)], ACT.Copy)
                if q == 3:
                    ins.then_inc(whi_done, 1)

            def tile(b, j, chunk=None):
                t = NJ * b + j
                a.wait_ge(tp_done, t + 1)
                if not (isinstance(t, int) and t < 2):
                    a.wait_ge(proj_done, t - 1)
                nc.scalar.activation(xnT[:, j % 2].rearrange("p k n -> p (k n)"), ps_t[j % 2][:, 0:D],
                                     ACT.Copy).then_inc(xnT_done, 1)
                if chunk is not None:
                    whi(chunk, j % GT)
                a.wait_ge(proj_done, t + 1)
                nc.scalar.activation(vs[:, 0, b, :, j, :],
                                     ps_p[j % 2][:, NE + NH:NP].rearrange("p (h d) -> p h d", h=NH),
                                     ACT.Copy).then_inc(vhi_done, 1)

            def z_exp(b):
                a.wait_ge(zneg_done, b + 1)
                if b >= 1:
                    a.wait_ge(zsplit_done, b)
                nc.scalar.activation(ez[:, ::-1], psz[0:NH, :, :].rearrange("p a n -> p (a n)"), ACT.Exp,
                                     bias=zst[:, 1:2], scale=SCALE,
                                     accum_out=zst[:, 2:3]).then_inc(zexp_done, 1)

            def z_hi(b):
                a.wait_ge(zn_done, b + 1)
                if b >= 1:
                    a.wait_ge(z_out, 16 * b)
                nc.scalar.activation(zhl[:, 0, 0:S], ez[:, :], ACT.Copy).then_inc(zhi_done, 1)

            a.wait_ge(eps_done, 1)
            std_group(0, 0)
            for b in range(B):
                for r in range(2):
                    n = 2 * b + r
                    for j in range(GT):
                        tile(b, GT * r + j, n if n < EARLY else None)
                    if n + 1 < 2 * B:
                        std_group(n + 1, 1 - r)
                z_exp(b)
                z_hi(b)

            a.wait_ge(rsub_done, 1)
            nc.scalar.activation(prob[:, :, :], prob[:, :, :], ACT.Exp).then_inc(route_exp, 1)

            def evac(b, g):
                n = NG * b + g
                a.wait_ge(conv_done, n + 1)
                if g == 0 and not (isinstance(b, int) and b == 0):
                    a.wait_ge(aotp_done, NJ * b)
                dst = ao[:, :, HG * HD * g:HG * HD * (g + 1)].rearrange("p i (h d) -> p h i d", h=HG)
                nc.scalar.activation(dst, ps_c[g % 2].rearrange("p (h i d) -> p h i d", h=HG, d=HD),
                                     ACT.Copy).then_inc(aoevac_done, 1)

            def turned(b):
                for i in range(NJ):
                    k = NJ * b + i
                    a.wait_ge(aotp_done, k + 1)
                    if not (isinstance(k, int) and k < 2):
                        a.wait_ge(wo_done, k - 1)
                    nc.scalar.activation(aoT[:, i % 2, :, ::-1],
                                         ps_t[i % 2][:, 0:D].rearrange("p (k n) -> p k n", k=KD), ACT.Copy).then_inc(aoT_done, 1)

            for g in range(NG):
                evac(0, g)
                if g == 0:
                    a.wait_ge(xn_out0, 16 * B)
                    a.wait_ge(xn_out1, 16 * B)
                    a.wait_ge(z_out, 16 * B)
                    a.wait_ge(proj_done, NT)
                whi(EARLY + g)
            turned(0)
            evac(1, 0)
            for g in range(1, NG):
                evac(1, g)
            with a.Fori(2, B) as b:
                turned(b - 1)
                evac(b, 0)
                for g in range(1, NG):
                    evac(b, g)
            turned(B - 1)
            a.wait_ge(list_done, 1)
            a.wait_ge(w8_out, 16)
            a.wait_ge(listmm_done, 8)
            for c in range(EARLY + MID, len(CHUNKS)):
                whi(c)

            def x_hi(n):
                a.wait_ge(xtp_done, n + 1)
                nc.scalar.activation(xT[:, 0].rearrange("p k n -> p (k n)"), bank6[:, :],
                                     ACT.Copy).then_inc(xhi_done, 1)

            def expert(n, last=False):
                for q in range(4):
                    a.wait_ge(g1_done, 4 * n + q + 1)
                    if not (isinstance(n, int) and n == 0):
                        a.wait_ge(glo_done, 4 * n + q - 3)
                    nc.scalar.activation(act[:, q, :], bank[q][:, :], ACT.Gelu)
                    nc.scalar.activation(gh[:, 2 * q:2 * q + 2, :].rearrange("p c n -> p (c n)"), bank[q][:, :],
                                         ACT.Gelu).then_inc(gelu_done, 1)
                if not last:
                    x_hi(n + 1)
                for m in range(2):
                    a.wait_ge(gate_done, n + 1)
                    a.wait_ge(g2_done, 2 * n + m + 1)
                    nc.scalar.activation(yt[:, m, :], ps_c[m][:, D:2 * D], ACT.Copy,
                                         scale=gate[:, m:m + 1]).then_inc(ylo_done, 1)

            x_hi(0)
            expert(0)
            with a.Fori(1, NTILE - 1) as n:
                expert(n)
            expert(NTILE - 1, last=True)

        @block.tensor
        def _(pe):
            def turn(t, r, j):
                pe.wait_ge(xn_done, t + 1)
                if not (isinstance(t, int) and t < 2):
                    pe.wait_ge(xnT_done, t - 1)
                for k in range(KD):
                    ins = nc.tensor.transpose(ps_t[j % 2][:, k * P:(k + 1) * P],
                                              xnb[:, r, j, k * P:(k + 1) * P], ident)
                ins.then_inc(tp_done, 1)

            def project(t, j):
                pe.wait_ge(xnT_done, t + 1)
                if not (isinstance(t, int) and t < 2):
                    pe.wait_ge(post_done, t - 1)
                for k in range(KD):
                    ins = nc.tensor.matmul(ps_p[j % 2][:, 0:NP], xnT[:, j % 2, k, :], wcat[:, k, :],
                                           start=(k == 0), stop=(k == KD - 1))
                ins.then_inc(proj_done, 1)

            pe.wait_ge(const_in, 32)
            pe.wait_ge(w_in, 16 * WEIGHTS)
            turn(0, 0, 0)
            for t in range(NT):
                if t % GT < GT - 1:
                    turn(t + 1, t // GT % 2, t % GT + 1)
                project(t, t)
                if t % GT == GT - 1 and t + 1 < NT:
                    turn(t + 1, (t + 1) // GT % 2, 0)
                if t % NJ == NJ - 1:
                    b = t // NJ
                    pe.wait_ge(lg_done, t + 1)
                    if b >= 1:
                        pe.wait_ge(zexp_done, b)
                    for j in range(NJ):
                        ins = nc.tensor.transpose(psz[0:NH, j // 4, (j % 4) * P:(j % 4 + 1) * P],
                                                  lg[:, j, NE:NE + NH], ident)
                    ins.then_inc(ztp_done, 1)

            def conv(b, g):
                n = NG * b + g
                pe.wait_ge(T_in[g % 2], 8 * (n - g % 2) + 16)
                if not (isinstance(n, int) and n < 2):
                    pe.wait_ge(aoevac_done, n - 1)
                for h in range(HG):
                    for k in range(NJ):
                        o = ps_c[g % 2][:, h * P + k * HD:(h + 1) * P]
                        for tl, vl in ((0, 0), (0, 1), (1, 0)):
                            v = vs[:, vl, b, HG * g + h, 0:NJ - k, :]
                            ins = nc.tensor.matmul(o, tz[:, g % 2, h, tl, (NJ - 1 - k) * P:(NJ - k) * P],
                                                   v.rearrange("p j d -> p (j d)"),
                                                   start=(k == 0 and tl + vl == 0),
                                                   stop=(k == NJ - 1 and tl == 1), skip_group_check=True)
                ins.then_inc(conv_done, 1)

            def attn_out(b):
                def turn_out(i):
                    k = NJ * b + i
                    if not (isinstance(k, int) and k < 2):
                        pe.wait_ge(aoT_done, k - 1)
                    for c in range(KD):
                        ins = nc.tensor.transpose(ps_t[i % 2][:, c * P:(c + 1) * P],
                                                  ao[:, i, c * P:(c + 1) * P], ident)
                    ins.then_inc(aotp_done, 1)

                pe.wait_ge(aoevac_done, NG * b + NG)
                turn_out(0)
                for i in range(NJ):
                    k = NJ * b + i
                    if i + 1 < NJ:
                        turn_out(i + 1)
                    pe.wait_ge(aoT_done, k + 1)
                    if not (isinstance(k, int) and k < 2):
                        pe.wait_ge(res_done, k - 1)
                    for c in range(KD):
                        ins = nc.tensor.matmul(ps_p[i % 2][:, 0:D], aoT[:, i % 2, c, :], wo[:, c, :],
                                               start=(c == 0), stop=(c == KD - 1))
                    ins.then_inc(wo_done, 1)

            def ranks():
                pe.wait_ge(mask_done, 1)
                m = maskb[:, :, :].rearrange("p t e -> p (t e)")
                nc.tensor.matmul(ps_rank, cb[:, C_UT:C_UT + P], m, start=True, stop=False,
                                 skip_group_check=True)
                for s in range(1, NT):
                    nc.tensor.matmul(ps_rank[:, s * NE:NT * NE], cb[:, C_ONE:C_ONE + P], m[:, 0:(NT - s) * NE],
                                     start=False, stop=(s == NT - 1), skip_group_check=True)
                nc.tensor.matmul(ps_cnt, cb[:, C_ONE:C_ONE + P], msum[:, :], start=True,
                                 stop=True).then_inc(cnt_done, 1)

            def list_part(u, first, last):
                pe.wait_ge(onehots, u + 1)
                for i in range(8):
                    s = 8 * (u % 2 if isinstance(u, int) else first) + i
                    ins = nc.tensor.matmul(ps_list, ohr[:, s, :], oha[:, s].rearrange("p v c -> p (v c)"),
                                           start=(u == 0 and i == 0) if isinstance(u, int) else False,
                                           stop=last and i == 7, skip_group_check=True)
                ins.then_inc(listmm_done, 1)

            pe.wait_ge(zexp_done, B)
            conv(0, 0)
            conv(0, 1)
            ranks()
            conv(0, 2)
            conv(0, 3)
            for b in range(1, B):
                conv(b, 0)
                if b < 3:
                    list_part(4 * (b - 1), 0, False)
                attn_out(b - 1)
                for g in range(1, NG):
                    conv(b, g)
                    if b < 3:
                        list_part(4 * (b - 1) + g, 0, b == 2 and g == 3)
            attn_out(B - 1)

            def x_turn(n, s):
                pe.wait_ge(g_in[s], 32 * (n // XS if isinstance(n, int) else n[0]) + 32)
                if not (isinstance(n, int) and n == 0):
                    pe.wait_ge(xlo_done, n if isinstance(n, int) else XS * n[0] + s)
                for k in range(KD):
                    for m in range(2):
                        ins = nc.tensor.transpose(bank6[:, k * TS + m * P:k * TS + (m + 1) * P],
                                                  xs[:, s, m, k * P:(k + 1) * P], ident)
                ins.then_inc(xtp_done, 1)

            def expert(n, nxt, s):
                e = pe.value_load(tei[0:1, bass.ds(n, 1)], min_val=0, max_val=NE - 1)
                pe.wait_ge(xlo_done, n + 1)
                for q in range(4):
                    if not (isinstance(n, int) and n == 0):
                        pe.wait_ge(gelu_done, 4 * n + q - 3)
                    for c in (2 * q, 2 * q + 1):
                        o = bank[q][:, (c % 2) * TS:(c % 2 + 1) * TS]
                        for k in range(KD):
                            for wl, xl in ((0, 0), (0, 1), (1, 0)):
                                ins = nc.tensor.matmul(o, w1s[:, e, wl, k, c * P:(c + 1) * P], xT[:, xl, k, :],
                                                       start=(k == 0 and wl + xl == 0),
                                                       stop=(k == KD - 1 and wl == 1))
                    ins.then_inc(g1_done, 1)
                if nxt is not None:
                    x_turn(nxt, s)
                for m in range(2):
                    if not (isinstance(n, int) and n == 0):
                        pe.wait_ge(y_done, 2 * n + m - 1)
                    for c in range(KH):
                        if m == 0 and c % 2 == 0:
                            pe.wait_ge(glo_done, 4 * n + c // 2 + 1)
                        nc.tensor.matmul(ps_c[m], gh[:, c, m * P:(m + 1) * P], w2s[:, e, c, :],
                                         start=(c == 0), stop=False, skip_group_check=True)
                        ins = nc.tensor.matmul(ps_c[m][:, 0:D], gl[:, c, m * P:(m + 1) * P], w2s[:, e, c, 0:D],
                                               start=False, stop=(c == KH - 1), skip_group_check=True)
                    ins.then_inc(g2_done, 1)

            pe.wait_ge(wlo_done, EARLY + MID)
            pe.wait_ge(wlate_done, LATE)
            pe.wait_ge(list_done, 1)
            pe.wait_ge(res_done, NT)
            pe.wait_ge(aoT_done, NT)
            x_turn(0, 0)
            for n in range(XS):
                expert(n, n + 1, (n + 1) % XS)
            with pe.Fori(1, NTILE // XS - 1) as i:
                for s in range(XS):
                    expert(XS * i + s, (i + (s + 1) // XS, ), (s + 1) % XS)
            for n in range(NTILE - XS, NTILE):
                expert(n, n + 1 if n + 1 < NTILE else None, (n + 1) % XS)

        @block.vector
        def _(v):
            def stats(n, r, j):
                if j == 0:
                    v.wait_ge(x_in[r], 16 * (n // 2 + 1))
                nc.vector.bn_stats(st[:, j, :], xin[:, r, j, :]).then_inc(stats_done, 1)

            def aggr(n, r, j):
                v.wait_ge(stats_done, GT * n + j + 1)
                nc.vector.bn_aggr(mv[:, r, j, :], st[:, j, :]).then_inc(aggr_done, 1)

            def norm(n, r):
                v.wait_ge(std_done, n + 1)
                nc.vector.reciprocal(rstd[:, r], std[:, r]).then_inc(rstd_done, 1)
                v.wait_ge(rstd_done, n + 1)
                if n >= 2:
                    v.wait_ge(xn_out[r], 16 * (n // 2))
                    v.wait_ge(tp_done, GT * (n - 1))
                for j in range(GT):
                    nc.vector.tensor_scalar(xnb[:, r, j, :], xin[:, r, j, :], mv[:, r, j, 0:1], rstd[:, r, j:j + 1],
                                            ALU.subtract, ALU.mult).then_inc(xn_done, 1)

            def post(t):
                b, j = t // NJ, t % NJ
                if j == 0 and b >= 1:
                    v.wait_ge(ztp_done, b)
                v.wait_ge(vhi_done, t + 1)
                nc.vector.tensor_copy(lg[:, j, :], ps_p[j % 2][:, 0:NE + NH]).then_inc(lg_done, 1)
                nc.vector.tensor_tensor(vs[:, 1, b, :, j, :],
                                        ps_p[j % 2][:, NE + NH:NP].rearrange("p (h d) -> p h d", h=NH),
                                        vs[:, 0, b, :, j, :], ALU.subtract).then_inc(post_done, 1)

            def z_part(b):
                v.wait_ge(lg_done, NJ * (b + 1))
                nc.vector.tensor_copy(lg8[:, NJ * b:NJ * (b + 1), :], lg[:, :, 0:NE]).then_inc(lg8_done, 1)
                v.wait_ge(ztp_done, b + 1)
                nc.vector.tensor_reduce(zst[:, 0:1], psz[0:NH, :, :].rearrange("p a n -> p (a n)"), AX.X,
                                        ALU.max).then_inc(zmax_done, 1)
                v.wait_ge(zmax_done, b + 1)
                nc.vector.tensor_scalar(zst[:, 1:2], zst[:, 0:1], -SCALE, None, ALU.mult).then_inc(zneg_done, 1)
                v.wait_ge(zexp_done, b + 1)
                nc.vector.reciprocal(zst[:, 3:4], zst[:, 2:3]).then_inc(zrec_done, 1)
                v.wait_ge(zrec_done, b + 1)
                nc.vector.tensor_scalar(ez[:, :], ez[:, :], zst[:, 3:4], None, ALU.mult).then_inc(zn_done, 1)
                v.wait_ge(zhi_done, b + 1)
                if b == 0:
                    v.wait_ge(zpad_done, 1)
                nc.vector.tensor_tensor(zhl[:, 1, 0:S], ez[:, :], zhl[:, 0, 0:S],
                                        ALU.subtract).then_inc(zsplit_done, 1)

            nc.vector.memset(eps[:, :], EPS).then_inc(eps_done, 1)
            for j in range(GT):
                stats(0, 0, j)
                aggr(0, 0, j)
            norm(0, 0)
            for n in range(2 * B):
                for j in range(GT):
                    if n + 1 < 2 * B:
                        stats(n + 1, 1 - n % 2, j)
                    post(GT * n + j)
                    if n + 1 < 2 * B:
                        aggr(n + 1, 1 - n % 2, j)
                if n + 1 < 2 * B:
                    norm(n + 1, 1 - n % 2)
                if n % 2 == 1:
                    z_part(n // 2)

            done = [0]

            def step(ins):
                done[0] += 1
                ins.then_inc(route, 1)
                v.wait_ge(route, done[0])

            def wide(col):
                return col.unsqueeze(2).to_broadcast([P, NT, NE])

            v.wait_ge(const_in, 32)
            v.wait_ge(lg8_done, B)
            c = [c32[:, i, :] for i in range(4)]
            step(nc.vector.tensor_reduce(c[0], lg8[:, :, :], AX.X, ALU.max))
            nc.vector.tensor_tensor(prob[:, :, :], lg8[:, :, :], wide(c[0]), ALU.subtract).then_inc(rsub_done, 1)
            v.wait_ge(route_exp, 1)
            step(nc.vector.tensor_reduce(c[1], prob[:, :, :], AX.X, ALU.add))
            step(nc.vector.reciprocal(c[2], c[1]))
            step(nc.vector.tensor_tensor(prob[:, :, :], prob[:, :, :], wide(c[2]), ALU.mult))
            ew = cf[:, C_EW:C_EW + NE].unsqueeze(1).to_broadcast([P, NT, NE])
            left = prob
            for oh in (oh1, oh2):
                step(nc.vector.tensor_reduce(c[0], left[:, :, :], AX.X, ALU.max))
                step(nc.vector.tensor_tensor(oh[:, :, :], left[:, :, :], wide(c[0]), ALU.is_equal))
                step(nc.vector.tensor_tensor(oh[:, :, :], oh[:, :, :], ew, ALU.mult))
                step(nc.vector.tensor_reduce(c[1], oh[:, :, :], AX.X, ALU.max))
                step(nc.vector.tensor_tensor(oh[:, :, :], oh[:, :, :], wide(c[1]), ALU.is_equal))
                if oh is oh1:
                    step(nc.vector.scalar_tensor_tensor(t8[:, :, :], oh1[:, :, :], -2.0, prob[:, :, :],
                                                        ALU.mult, ALU.add))
                    left = t8
            step(nc.vector.tensor_tensor(rank[:, :, :], oh1[:, :, :], oh2[:, :, :], ALU.add))
            step(nc.vector.tensor_copy(maskb[:, :, :], rank[:, :, :]))
            with nc.allow_low_precision("sums of at most 32 ones are exact"):
                step(nc.vector.tensor_reduce(msum[:, :], rank[:, :, :].rearrange("p t e -> p e t"), AX.X, ALU.add))
            nc.vector.tensor_tensor(t8[:, :, :], rank[:, :, :], prob[:, :, :], ALU.mult).then_inc(mask_done, 1)

            v.wait_ge(cnt_done, 1)
            e = [e8[:, i, :] for i in range(6)]
            step(nc.vector.tensor_scalar(e8i[:, 0, :], ps_cnt, float(TS - 1), None, ALU.add))
            step(nc.vector.tensor_scalar(e8i[:, 1, :], e8i[:, 0, :], 8, None, ALU.arith_shift_right))
            step(nc.vector.tensor_copy(e[0], e8i[:, 1, :]))
            step(nc.vector.memset(e[1], 1.0))
            step(nc.vector.tensor_tensor_scan(e[2], e[1], e[0], 0.0, ALU.mult, ALU.add))
            step(nc.vector.tensor_tensor(e[3], e[2], e[0], ALU.subtract))
            step(nc.vector.tensor_scalar(e[4], e[3], float(TS), None, ALU.mult))
            step(nc.vector.tensor_tensor(rank[:, :, :], ps_rank.rearrange("p (t e) -> p t e", e=NE),
                                         e[4].unsqueeze(1).to_broadcast([P, NT, NE]), ALU.add))
            for i, oh in enumerate((oh1, oh2)):
                step(nc.vector.tensor_tensor(oh[:, :, :], oh[:, :, :], rank[:, :, :], ALU.mult))
                step(nc.vector.tensor_reduce(posf[:, i, :], oh[:, :, :], AX.X, ALU.add))
            pf, pi = (z[:, :, :].rearrange("p a t -> p (a t)") for z in (posf, posi))
            step(nc.vector.tensor_copy(pi, pf))
            step(nc.vector.tensor_scalar(pi, pi, 7, None, ALU.arith_shift_right))
            step(nc.vector.tensor_copy(colA[:, :], pi))
            step(nc.vector.scalar_tensor_tensor(colR[:, :], colA[:, :], -float(P), pf, ALU.mult, ALU.add))
            step(nc.vector.memset(ge9[:, :, 0:1], 1.0))
            step(nc.vector.memset(ge9[:, :, NE:NE + 1], 0.0))
            step(nc.vector.tensor_tensor(
                ge9[:, :, 1:NE], cf[:, C_S:C_S + NTILE * (NE - 1)].rearrange("p (s e) -> p s e", e=NE - 1),
                e8[:, 2, 0:NE - 1].unsqueeze(1).to_broadcast([P, NTILE, NE - 1]), ALU.is_ge))
            step(nc.vector.tensor_tensor(teoh[:, :, :], ge9[:, :, 0:NE], ge9[:, :, 1:NE + 1], ALU.subtract))
            step(nc.vector.tensor_reduce(tef[:, :], ge9[:, :, 1:NE], AX.X, ALU.add))
            step(nc.vector.tensor_copy(tei[:, :], tef[:, :]))

            def one_hots(u, slot, k0):
                if u >= 2:
                    v.wait_ge(listmm_done, u - 1)
                for i in range(8):
                    s, k = 8 * slot + i, k0 + i
                    nc.vector.tensor_scalar(ohr[:, s, :], cb[:, C_IR:C_IR + P], colR[:, k:k + 1], None,
                                            ALU.is_equal)
                    nc.vector.tensor_scalar(oha[:, s, 0, :], cb[:, C_IA:C_IA + NCOL], colA[:, k:k + 1],
                                            cf[:, C_TP1 + k:C_TP1 + k + 1], ALU.is_equal, ALU.mult)
                    ins = nc.vector.tensor_scalar(oha[:, s, 1, :], cb[:, C_IA:C_IA + NCOL], colA[:, k:k + 1],
                                                  cf[:, C_P:C_P + 1], ALU.is_equal, ALU.mult)
                ins.then_inc(onehots, 1)

            def residual(b):
                v.wait_ge(xrb_done, b + 1)
                for i in range(NJ):
                    v.wait_ge(wo_done, NJ * b + i + 1)
                    nc.vector.tensor_tensor(xr[:, i, :], ps_p[i % 2][:, 0:D], xr[:, i, :],
                                            ALU.add).then_inc(res_done, 1)

            for u in range(8):
                one_hots(u, u % 2, 8 * u)
                if u % 4 == 0:
                    residual(u // 4)
            v.wait_ge(listmm_done, 8)
            step(nc.vector.tensor_copy(idf[:, :, :].rearrange("p v c -> p (v c)"), ps_list))
            step(nc.vector.scalar_tensor_tensor(idf[:, 1, :], idf[:, 0, :], float(P), idf[:, 1, :],
                                                ALU.mult, ALU.add))
            step(nc.vector.tensor_scalar(idf[:, 0, :], idf[:, 0, :], 0.0, None, ALU.is_equal))
            step(nc.vector.tensor_tensor(idf[:, 0, :], idf[:, 0, :], cf[:, C_PAD:C_PAD + NCOL], ALU.mult))
            step(nc.vector.tensor_tensor(idf[:, 1, :], idf[:, 1, :], idf[:, 0, :], ALU.add))
            nc.vector.tensor_scalar(idt[:, :], idf[:, 1, :], -float(P), None, ALU.add).then_inc(list_done, 1)
            residual(2)
            residual(3)
            for ch in range(EARLY + MID, len(CHUNKS)):
                hi, lo, s = w_split(ch)
                v.wait_ge(stage_in[ch % 2], 16 * (ch // 2 + 1))
                v.wait_ge(whi_done, ch + 1)
                nc.vector.tensor_tensor(lo, s, hi, ALU.subtract).then_inc(wlate_done, 1)

            def x_lo(n):
                v.wait_ge(xhi_done, n + 1)
                nc.vector.tensor_tensor(xT[:, 1].rearrange("p k n -> p (k n)"), bank6[:, :],
                                        xT[:, 0].rearrange("p k n -> p (k n)"), ALU.subtract).then_inc(xlo_done, 1)

            def gates(n, k, s):
                v.wait_ge(g_in[s], 32 * k + 32)
                nc.vector.tensor_tensor(g8[:, :, :], xs[:, s, :, D:ROW],
                                        teoh[:, bass.ds(n, 1), :].to_broadcast([P, 2, NE]),
                                        ALU.mult).then_inc(g8_done, 1)
                v.wait_ge(g8_done, n + 1)
                nc.vector.tensor_reduce(gate[:, :], g8[:, :, :], AX.X, ALU.add).then_inc(gate_done, 1)

            def expert(n, nxt, s):
                for q in range(4):
                    v.wait_ge(gelu_done, 4 * n + q + 1)
                    nc.vector.tensor_tensor(gl[:, 2 * q:2 * q + 2, :].rearrange("p c n -> p (c n)"), act[:, q, :],
                                            gh[:, 2 * q:2 * q + 2, :].rearrange("p c n -> p (c n)"),
                                            ALU.subtract).then_inc(glo_done, 1)
                if nxt is not None:
                    x_lo(nxt[0])
                for m in range(2):
                    v.wait_ge(ylo_done, 2 * n + m + 1)
                    v.wait_ge(gate_done, n + 1)
                    if not (isinstance(n, int) and n == 0):
                        v.wait_ge(acc_out, 32 * n + 16 * m - 16)
                    nc.vector.scalar_tensor_tensor(y[:, m, :], ps_c[m][:, 0:D], gate[:, m:m + 1], yt[:, m, :],
                                                   ALU.mult, ALU.add).then_inc(y_done, 1)
                if nxt is not None:
                    gates(nxt[0], nxt[1], s)

            x_lo(0)
            gates(0, 0, 0)
            for n in range(XS):
                expert(n, (n + 1, (n + 1) // XS), (n + 1) % XS)
            with v.Fori(1, NTILE // XS - 1) as i:
                for s in range(XS):
                    expert(XS * i + s, (XS * i + s + 1, i + (s + 1) // XS), (s + 1) % XS)
            for n in range(NTILE - XS, NTILE):
                expert(n, (n + 1, (n + 1) // XS) if n + 1 < NTILE else None, (n + 1) % XS)


def kernel(**inputs):
    import numpy as np
    import ml_dtypes
    import concourse.bacc as bacc
    from concourse import mybir as mb
    from concourse.bass_utils import run_bass_kernel_spmd as run

    cf = np.zeros((P, C_F), np.float32)
    cf[:, C_ID:C_ID + P] = np.eye(P)
    cf[:, C_TP1:C_TP1 + 2 * NT] = np.arange(2 * NT) % NT + 1
    cf[:, C_P] = np.arange(P)
    cf[:, C_EW:C_EW + NE] = NE - np.arange(NE)
    cf[:, C_S:C_S + NTILE * (NE - 1)] = np.repeat(np.arange(NTILE), NE - 1)
    cf[:, C_PAD:C_PAD + NCOL] = P + TOK + (np.arange(NCOL) % 2)[None, :] * P + np.arange(P)[:, None]
    cb = np.zeros((P, C_B), np.float32)
    cb[:, C_UT:C_UT + P] = np.triu(np.ones((P, P)), 1)
    cb[:, C_ONE:C_ONE + P] = 1
    cb[:, C_IR:C_IR + P] = np.arange(P)
    cb[:, C_IA:C_IA + NCOL] = np.arange(NCOL)
    cb = cb.astype(ml_dtypes.bfloat16)

    def laid(a, *order):
        a = np.asarray(a)
        return np.ascontiguousarray(a.transpose(order) if order else a)

    arrays = {
        "x": laid(inputs["L0_attn_x"]).reshape(TOK, D),
        "routerT": laid(inputs["L0_ffn_router_w"], 1, 0),
        "waT": laid(inputs["L0_attn_W_A"], 1, 0),
        "wvT": laid(inputs["L0_attn_W_V"], 1, 0),
        "woT": laid(inputs["L0_attn_W_O"], 1, 0),
        "b_o": laid(inputs["L0_attn_b_O"]),
        "w1T": laid(inputs["L0_ffn_w1"], 0, 2, 1),
        "w2T": laid(inputs["L0_ffn_w2"], 0, 2, 1),
        "const_f": cf,
        "const_b": cb,
        "zeros": np.zeros((PADROWS, ROW), np.float32),
    }
    nc = bacc.Bacc("TRN2", target_bir_lowering=False, num_devices=1)
    args = [nc.dram_tensor(n, a.shape, mb.dt.from_np(a.dtype), kind="ExternalInput").ap() for n, a in arrays.items()]
    args.append(nc.dram_tensor("out", (TOK + PADROWS, D), F32, kind="ExternalOutput").ap())
    build(nc, *args)
    r = run(nc, [arrays], core_ids=[0])
    return r.results[0]["out"][0:TOK].reshape(B, S, D)
```

```python
from contextlib import ExitStack

import concourse.bass as bass
from concourse import mybir

F32 = mybir.dt.float32
BF16 = mybir.dt.bfloat16
I32 = mybir.dt.int32
U32 = mybir.dt.uint32
ALU = mybir.AluOpType
ACT = mybir.ActivationFunctionType
AX = mybir.AxisListType

P = 128
B, S, D = 4, 1024, 256
NH, HD = 16, 16
NE, H = 8, 1024
TOK = B * S
NT = TOK // P
NJ = S // P
KD = D // P
KH = H // P
NP = NE + NH + D
TS = 256
NTILE = (2 * TOK) // TS + NE - 1
NCOL = NTILE * TS // P
ROW = D + NE
PADROWS = 2 * P
NZ = S + P
HG = NH // NJ
NU = B * NJ
LATE0 = 24
PIECE = 1024
NPIECE = NE * 2 * KD * H // PIECE
NSTG = 4
NB_E = 8
SCALE = float(HD) ** -0.5
EPS = 1e-5

C_ID, C_P, C_EW, C_S, C_PAD = 0, 128, 129, 137, 137 + NTILE
C_F = C_PAD + NCOL
C_UT, C_ONE, C_IR, C_IA = 0, 128, 256, 384
C_B = C_IA + NCOL


def build(nc, x, routerT, waT, wvT, woT, b_o, w1T, w2T, const_f, const_b, zeros, out):
    x_b = x.rearrange("(b t p) d -> b p t d", p=P, t=NJ)
    out_pair = out[0:TOK, :].rearrange("(g t p) d -> g p t d", p=P, t=2)
    w1_v = w1T.rearrange("e (k p) h -> e k p h", p=P)
    w2_v = w2T.rearrange("e (f c p) d -> e f p c d", p=P, f=2)

    with ExitStack() as ctx:
        xn_dram = nc.dram_tensor("xn_table", [TOK + PADROWS, ROW], F32).ap()
        z_dram = nc.dram_tensor("z_reversed", [B, NJ, HG, 2, NZ], BF16).ap()
        v_dram = nc.dram_tensor("v_halves", [B, P, 2 * NH * NJ * HD], BF16).ap()
        xn_rows = xn_dram[0:TOK, :].rearrange("(b t p) d -> b p t d", p=P, t=NJ)
        xn_w8 = xn_dram[0:TOK, :].rearrange("(t p) d -> p t d", p=P)

        cursor = [16512]

        def sb(name, shape, dt, zone=None):
            size = 4 if dt in (F32, I32, U32) else 2
            for n in shape[1:]:
                size *= n
            c = cursor if zone is None else zone
            t = nc.alloc_sbuf_tensor_at(name, shape, dt, offset=c[0])
            c[0] += (size + 31) // 32 * 32
            return t

        w1s = sb("w1s", [P, NE, 2, KD, H], BF16)
        w2_at = cursor[0]
        w2s = sb("w2s", [P, NE, KH, 2 * D], BF16)
        zone = [w2_at + 4 * KH * 2 * D * 2]
        xw = sb("x_normed", [P, NT, D], F32, zone)
        assert zone[0] == cursor[0]

        zone = [cursor[0]]
        stage = sb("w_stage", [P, NSTG, PIECE], F32)
        tz = sb("toeplitz", [P, 2, HG, 2, S], BF16, zone)
        assert zone[0] == cursor[0]

        zone = [cursor[0]]
        vb = [sb(f"v_split{i}", [P, 2, NH, NJ, HD], BF16, zone) for i in range(3)]
        cursor[0] += 2 * NH * NJ * HD * 2
        ao_acc = sb("attn_conv", [P, NJ, D], F32)
        ao = sb("attn_out", [P, NJ, D], F32)
        assert zone[0] == cursor[0]

        zone = [cursor[0]]
        ez_at = cursor[0]
        ez = sb("z_exp", [NH, S], F32, zone)
        ohr = nc.alloc_sbuf_tensor_at("onehot_r", [P, 2 * NB_E, P], BF16, offset=ez_at)
        zhl = sb("z_split", [NH, 2, NZ], BF16, zone)
        xnT = sb("xnT", [P, 2, KD, P], F32, zone)
        wcat = sb("w_cat", [P, KD, NP], F32, zone)
        lg = sb("logits", [P, NT, NE + NH], F32, zone)
        prob = sb("prob", [P, NT, NE], F32, zone)
        t8 = sb("route_t8", [P, NT, NE], F32, zone)
        oh1 = sb("onehot1", [P, NT, NE], F32, zone)
        oh2 = sb("onehot2", [P, NT, NE], F32, zone)
        rank = sb("rank", [P, NT, NE], F32, zone)
        maskb = sb("mask_bf", [P, NT, NE], BF16, zone)
        c32 = sb("cols32", [P, 4, NT], F32, zone)
        posf = sb("pos_f", [P, NT, 2], F32, zone)
        posi = sb("pos_i", [P, NT, 2], I32, zone)
        ohe = sb("onehot_a", [P, 2 * NB_E, NCOL], BF16, zone)
        oha = sb("onehot_tp", [P, 2 * NB_E, 2, NCOL], BF16, zone)
        ge9 = sb("tile_ge", [P, NTILE, NE + 1], F32, zone)
        idf = sb("list_f", [P, 2, NCOL], F32, zone)
        front_end = zone[0]
        zone = [cursor[0]]
        xs = sb("x_sorted", [P, 2, 2, ROW], F32, zone)
        xT = sb("xT_split", [P, 2, KD, TS], BF16, zone)
        act = sb("gelu", [P, 2, 2 * TS], F32, zone)
        gh = sb("gelu_hi", [P, KH, TS], BF16, zone)
        gl = sb("gelu_lo", [P, KH, TS], BF16, zone)
        yt = sb("y_lo", [P, 2, D], F32, zone)
        y = sb("y", [P, 2, D], F32, zone)
        at = sb("attn_rows", [P, 4, D], F32, zone)
        wo = sb("w_o", [P, KD, D], F32, zone)
        bo = sb("b_o", [P, D], F32, zone)
        cursor[0] = max(front_end, zone[0])

        aoT = sb("attn_outT", [P, KD, P], F32)
        cf = sb("const_f", [P, C_F], F32)
        cb = sb("const_b", [P, C_B], BF16)
        st = sb("stats", [P, NJ, 6], F32)
        mv = sb("mean_var", [P, NT, 2], F32)
        std = sb("std", [P, NT], F32)
        rstd = sb("rstd", [P, NT], F32)
        zst = sb("z_stats", [NH, 4], F32)
        eps = sb("eps", [P, 1], F32)
        colA = sb("place_col", [P, 2 * NT], F32)
        colR = sb("place_row", [P, 2 * NT], F32)
        e8 = sb("per_expert", [P, 6, NE], F32)
        e8i = sb("per_expert_i", [P, 2, NE], I32)
        msum = sb("mask_sum", [P, NE], BF16)
        teoh = sb("tile_onehot", [P, NTILE, NE], F32)
        tef = sb("tile_expert_f", [P, NTILE], F32)
        tei = sb("tile_expert", [P, NTILE], I32)
        idt = sb("list", [P, NCOL], U32)
        idxs = sb("gather_index", [P, 4, 2], U32)
        g8 = sb("gate8", [P, 2, NE], F32)
        gate = sb("gate", [P, 2], F32)
        held = sb("held", [P, 5], F32)
        assert cursor[0] <= nc.sbuf_usable_end, cursor[0]

        bank = [ctx.enter_context(nc.psum_tensor(f"bank{i}", [P, 512], F32)) for i in range(4)]
        psz = ctx.enter_context(nc.psum_tensor("bank45", [P, 2, 512], F32))
        bank6 = ctx.enter_context(nc.psum_tensor("bank6", [P, 512], F32))
        bank7 = ctx.enter_context(nc.psum_tensor("bank7", [P, 512], F32))
        ps_t, ps_p = bank[0:2], bank[2:4]
        ps_rank = bank6[:, 0:NT * NE]
        ps_cnt = bank7[:, 256:256 + NE]
        ps_list = bank7[:, 0:2 * NCOL]
        ps_h = [bank[0], bank[1], bank[2], bank[0]]
        ps_c = bank[3][:, 0:HG * P]
        ps_y = [psz[:, 0, :], psz[:, 1, :]]
        ps_x = bank6
        ps_ot, ps_o = bank7[:, 0:D], bank7[:, D:2 * D]

        ident = cf[:, C_ID:C_ID + P]

        def sems(text):
            return [ctx.enter_context(nc.semaphore(n)) for n in text.split()]

        const_in, w_in, wo_in, pads_out, x_out, xn_out, z_out, w8_out = sems(
            "const_in w_in wo_in pads_out x_out xn_out z_out w8_out")
        x_in = sems("x_in0 x_in1 x_in2 x_in3")
        stage_in = sems("stage_in0 stage_in1 stage_in2 stage_in3")
        T_in = sems("T_in0 T_in1")
        g_in = sems("g_in0 g_in1")
        v_out = sems("v_out1 v_out2 v_out3")
        v_in, acc_out = sems("v_in acc_out")
        eps_done, zpad_done, held_done, stats_done, aggr_done, std_done, rstd_done, xn_done = sems(
            "eps_done zpad_done held_done stats_done aggr_done std_done rstd_done xn_done")
        tp_done, xnT_done, proj_done, lg_done, vhi_done, post_done, whi_done, wpool_done, wdve_done = sems(
            "tp_done xnT_done proj_done lg_done vhi_done post_done whi_done wpool_done wdve_done")
        ztp_done, zmax_done, zneg_done, zexp_done, zrec_done, zn_done, zhi_done, zsplit_done = sems(
            "ztp_done zmax_done zneg_done zexp_done zrec_done zn_done zhi_done zsplit_done")
        route, route_exp, rsub_done, mask_done, cnt_done, oneh_done, onehots, listmm_done, list_done = sems(
            "route route_exp rsub_done mask_done cnt_done oneh_done onehots listmm_done list_done")
        idx_done, xtp_done, xhi_done, xlo_done, g1_done, gelu_done, glo_done, g2_done, ylo_done, y_done = sems(
            "idx_done xtp_done xhi_done xlo_done g1_done gelu_done glo_done g2_done ylo_done y_done")
        g8_done, gate_done, conv_done, aoevac_done, aocur_done, aotp_done, aoT_done, wo_done, at_done = sems(
            "g8_done gate_done conv_done aoevac_done aocur_done aotp_done aoT_done wo_done at_done")
        V_SLOT = (0, 1, 2, 1)

        def w_piece(c):
            m, e, f = c // (NPIECE // 2), c % (NPIECE // 2) // 2, c % 2
            s = stage[:, c % NSTG, :]
            if m == 0:
                return w1s[:, e, 0, f], w1s[:, e, 1, f], s, w1_v[e, f]
            half = w2s[:, e, f * KH // 2:(f + 1) * KH // 2]
            return half[:, :, 0:D], half[:, :, D:2 * D], s.rearrange("p (c d) -> p c d", d=D), w2_v[e, f]

        def on_dve(c):
            return c % NSTG == NSTG - 1 and c < LATE0

        def wait_lo(eng, c):
            if on_dve(c):
                eng.wait_ge(wdve_done, c // NSTG + 1)
            else:
                eng.wait_ge(wpool_done, sum(not on_dve(i) for i in range(c + 1)))

        def piece_at(t):
            return 3 * (t // 4) + t % 4 if t % 4 < 3 else None

        def acc_before(n, b, j):
            if isinstance(b, int) and b == 0:
                return 2 * n
            return 20 * b - 4 + 2 * j + j // 2

        def for_tiles(eng, run):
            for j in range(NJ):
                run(j, 0, j, True, False)
            with eng.Fori(1, B) as b:
                for j in range(NJ):
                    run(NJ * b + j, b, j, True, True)
            for n in range(NU, NTILE):
                run(n, B, n - NU, False, True)

        block = ctx.enter_context(nc.Block())

        @block.sync
        def _(sp):
            sp.dma_start(xw[:, 0:NJ, :], x_b[0]).then_inc(x_in[0], 16)
            sp.dma_start(cf[:, :], const_f).then_inc(const_in, 16)
            sp.dma_start(xw[:, NJ:2 * NJ, :], x_b[1]).then_inc(x_in[1], 16)
            sp.dma_start(wcat[:, :, 0:NE], routerT.rearrange("(k p) n -> p k n", p=P)).then_inc(w_in, 16)
            sp.dma_start(wcat[:, :, NE:NE + NH], waT.rearrange("(k p) n -> p k n", p=P)).then_inc(w_in, 16)
            sp.dma_start(wcat[:, :, NE + NH:NP], wvT.rearrange("(k p) n -> p k n", p=P)).then_inc(w_in, 16)
            sp.dma_start(cb[:, :], const_b).then_inc(const_in, 16)
            sp.dma_start(xw[:, 2 * NJ:3 * NJ, :], x_b[2]).then_inc(x_in[2], 16)
            sp.dma_start(xw[:, 3 * NJ:4 * NJ, :], x_b[3]).then_inc(x_in[3], 16)
            sp.dma_start(xn_dram[TOK:TOK + PADROWS, :], zeros).then_inc(pads_out, 16)
            sp.dma_start(out[TOK:TOK + PADROWS, :], zeros[:, 0:D]).then_inc(x_out, 16)

            def rows_out(b):
                sp.wait_ge(xn_done, NJ * (b + 1))
                sp.dma_start(xn_rows[b, :, :, 0:D], xw[:, NJ * b:NJ * (b + 1), :]).then_inc(xn_out, 16)

            def z_write(b):
                sp.wait_ge(zsplit_done, b + 1)
                sp.dma_start(z_dram[b].rearrange("u h l s -> (u h) l s"), zhl[:, :, :]).then_inc(z_out, 16)

            rows_out(0)
            for b in range(B):
                if b + 1 < B:
                    rows_out(b + 1)
                if b >= 1:
                    z_write(b - 1)
                    sp.wait_ge(post_done, NJ * (b + 1))
                    sp.dma_start(v_dram[b], vb[V_SLOT[b]][:, :, :, :, :].rearrange("p l h j d -> p (l h j d)")
                                 ).then_inc(v_out[b - 1], 16)
            sp.wait_ge(mask_done, 1)
            sp.dma_start(xn_w8[:, :, D:ROW], t8[:, :, :]).then_inc(w8_out, 16)
            z_write(B - 1)

            def toeplitz(u, b, j):
                src = z_dram[b, j]
                src = bass.AP(src.tensor, src.offset, [[1, P], [NZ, HG * 2], [1, S]])
                sp.dma_start(tz[:, j % 2].rearrange("p h l s -> p (h l) s"), src).then_inc(T_in[j % 2], 16)

            for c in range(NPIECE - NSTG, NPIECE):
                wait_lo(sp, c)
            sp.wait_ge(z_out, 16 * B)
            toeplitz(0, 0, 0)
            toeplitz(1, 0, 1)
            sp.wait_ge(list_done, 1)
            sp.dma_start(wo[:, :, :], woT.rearrange("(k p) n -> p k n", p=P)).then_inc(wo_in, 16)
            sp.dma_start(bo[:, :], b_o.partition_broadcast(P)).then_inc(wo_in, 16)
            sp.dma_start(out[0:TOK, :].rearrange("(a r) d -> a (r d)", a=P),
                         x.rearrange("(a r) d -> a (r d)", a=P)).then_inc(x_out, 16)

            def reload(b, j, last):
                sp.wait_ge(conv_done, NJ * b + j + 1)
                if j + 2 < NJ:
                    toeplitz(NJ * b + j + 2, b, j + 2)
                elif not last:
                    toeplitz(NJ * b + j + 2, b + 1, j + 2 - NJ)
                if j == NJ - 1 and not last:
                    sp.dma_start(vb[0][:, :, :, :, :].rearrange("p l h j d -> p (l h j d)"),
                                 v_dram[b + 1]).then_inc(v_in, 16)

            for b in range(B - 1):
                sp.wait_ge(v_out[b], 16)
            with sp.Fori(0, B - 1) as b:
                for j in range(NJ):
                    reload(b, j, False)
            for j in range(NJ - 2):
                reload(B - 1, j, True)

        @block.gpsimd
        def _(pool):
            nc.gpsimd.memset(held[:, :], 0.0).then_inc(held_done, 1)
            nc.gpsimd.memset(zhl[:, :, S:NZ], 0.0).then_inc(zpad_done, 1)
            for c in range(NPIECE):
                if not on_dve(c):
                    hi, lo, s, _src = w_piece(c)
                    pool.wait_ge(whi_done, c + 1)
                    nc.gpsimd.tensor_tensor(lo, s, hi, ALU.subtract).then_inc(wpool_done, 1)

            def hold(i, n):
                if not isinstance(n, int):
                    nc.gpsimd.tensor_tensor(held[:, i:i + 1], held[:, 4:5], held[:, 4:5], ALU.add)

            def gather(n, s, si):
                nc.gpsimd.tensor_copy(idxs[:, si, :], idt[:, bass.ds(2 * n, 2)]).then_inc(idx_done, 1)
                pool.wait_ge(idx_done, n + 1)
                hold(0, n)
                for m in range(2):
                    nc.gpsimd.indirect_dma_start(
                        out=xs[:, s, m, :], out_offset=None, in_=xn_dram[:, :],
                        in_offset=bass.IndirectOffsetOnAxis(ap=idxs[:, si, m:m + 1], axis=0),
                    ).then_inc(g_in[s], 16)

            def tile(n, b, j, conv, proj):
                before = acc_before(n, b, j)
                if not isinstance(n, int) or n + 2 < NTILE:
                    pool.wait_ge(gate_done, n + 1)
                    pool.wait_ge(xtp_done, n + 1)
                    gather(n + 2, j % 2, (j + 2) % 4)
                for m in range(2):
                    pool.wait_ge(y_done, 2 * n + m + 1)
                    if not (isinstance(n, int) and n == 0 and m == 0):
                        pool.wait_ge(acc_out, 16 * (before + m))
                    hold(1 + m, n)
                    nc.gpsimd.indirect_dma_start(
                        out=out[:, :], out_offset=bass.IndirectOffsetOnAxis(ap=idxs[:, j % 4, m:m + 1], axis=0),
                        in_=y[:, m, :], in_offset=None, compute_op=ALU.add,
                    ).then_inc(acc_out, 16)
                if proj and j % 2 == 1:
                    add_rows(b, j, before + 2)

            def add_rows(b, j, before):
                pool.wait_ge(at_done, NJ * (b - 1) + j + 1)
                pool.wait_ge(acc_out, 16 * before)
                hold(3, b)
                k = (j - 1) % 4
                nc.gpsimd.dma_start(out_pair[(NJ // 2) * (b - 1) + j // 2], at[:, k:k + 2, :],
                                    accum_op=ALU.add).then_inc(acc_out, 16)

            pool.wait_ge(held_done, 1)
            pool.wait_ge(list_done, 1)
            pool.wait_ge(z_out, 16 * B)
            pool.wait_ge(xn_out, 16 * B)
            pool.wait_ge(w8_out, 16)
            pool.wait_ge(pads_out, 16)
            gather(0, 0, 0)
            gather(1, 1, 1)
            pool.wait_ge(x_out, 32)
            for_tiles(pool, tile)
            add_rows(B, NJ - 1, acc_before(NTILE, B, NTILE - NU))
            pool.wait_ge(acc_out, 16 * (acc_before(NTILE, B, NTILE - NU) + 1))

        @block.scalar
        def _(a):
            def load_piece(c):
                if c >= NSTG:
                    wait_lo(a, c - NSTG)
                _hi, _lo, s, src = w_piece(c)
                a.dma_start(s, src).then_inc(
                    stage_in[c % NSTG], 16)

            def split_hi(c):
                hi, _lo, s, _src = w_piece(c)
                a.wait_ge(stage_in[c % NSTG], 16 * (c // NSTG + 1))
                nc.scalar.activation(hi, s, ACT.Copy).then_inc(whi_done, 1)

            def std_of(b):
                a.wait_ge(aggr_done, NJ * (b + 1))
                nc.scalar.activation(std[:, NJ * b:NJ * (b + 1)], mv[:, NJ * b:NJ * (b + 1), 1], ACT.Sqrt,
                                     bias=eps[:, :]).then_inc(std_done, 1)

            def z_exp(b):
                a.wait_ge(zneg_done, b + 1)
                if b >= 1:
                    a.wait_ge(zsplit_done, b)
                nc.scalar.activation(ez[:, ::-1], psz[0:NH, :, :].rearrange("p a n -> p (a n)"), ACT.Exp,
                                     bias=zst[:, 1:2], scale=SCALE,
                                     accum_out=zst[:, 2:3]).then_inc(zexp_done, 1)

            def z_hi(b):
                a.wait_ge(zn_done, b + 1)
                if b >= 1:
                    a.wait_ge(z_out, 16 * b)
                nc.scalar.activation(zhl[:, 0, 0:S], ez[:, :], ACT.Copy).then_inc(zhi_done, 1)

            a.wait_ge(eps_done, 1)
            a.wait_ge(x_in[0], 16)
            for c in range(NSTG - 1):
                load_piece(c)
            std_of(0)
            std_of(1)
            for t in range(NT):
                b, j = t // NJ, t % NJ
                a.wait_ge(tp_done, t + 1)
                if t >= 2:
                    a.wait_ge(proj_done, t - 1)
                nc.scalar.activation(xnT[:, t % 2].rearrange("p k n -> p (k n)"), ps_t[t % 2][:, 0:D],
                                     ACT.Copy).then_inc(xnT_done, 1)
                c = piece_at(t)
                if c is not None:
                    split_hi(c)
                    if c >= 1:
                        load_piece(c + 2)
                a.wait_ge(proj_done, t + 1)
                if j == 0 and b == 3:
                    a.wait_ge(v_out[0], 16)
                nc.scalar.activation(vb[V_SLOT[b]][:, 0, :, j, :],
                                     ps_p[t % 2][:, NE + NH:NP].rearrange("p (h d) -> p h d", h=NH),
                                     ACT.Copy).then_inc(vhi_done, 1)
                if j == 2 and b >= 1:
                    z_exp(b - 1)
                if j == 5 and b >= 1:
                    z_hi(b - 1)
                if j == NJ - 1 and b + 2 < B:
                    std_of(b + 2)
            a.wait_ge(xn_out, 16 * B)
            split_hi(LATE0)
            load_piece(LATE0 + 2)
            z_exp(B - 1)
            a.wait_ge(rsub_done, 1)
            nc.scalar.activation(prob[:, :, :], prob[:, :, :], ACT.Exp).then_inc(route_exp, 1)
            z_hi(B - 1)
            for c in range(LATE0 + 1, NPIECE):
                split_hi(c)
                if c + 2 < NPIECE:
                    load_piece(c + 2)
            for u in range(2 * NT // NB_E):
                a.wait_ge(oneh_done, u + 1)
                if u >= 2:
                    a.wait_ge(listmm_done, u - 1)
                k = NB_E * (u % 2)
                nc.scalar.activation(oha[:, k:k + NB_E, 1, :], ohe[:, k:k + NB_E, :], ACT.Copy,
                                     scale=cf[:, C_P:C_P + 1])
                for i in range(0, NB_E, 2):
                    t = (NB_E * u + i) // 2
                    ins = nc.scalar.activation(oha[:, k + i:k + i + 2, 0, :], ohe[:, k + i:k + i + 2, :],
                                               ACT.Copy, scale=float(t + 1))
                ins.then_inc(onehots, 1)

            def x_hi(n):
                a.wait_ge(xtp_done, n + 1)
                nc.scalar.activation(xT[:, 0].rearrange("p k n -> p (k n)"), ps_x[:, :],
                                     ACT.Copy).then_inc(xhi_done, 1)

            def tile(n, b, j, conv, proj):
                for q in range(4):
                    a.wait_ge(g1_done, 4 * n + q + 1)
                    if not (isinstance(n, int) and n == 0 and q < 2):
                        a.wait_ge(glo_done, 4 * n + q - 1)
                    nc.scalar.activation(act[:, q % 2, :], ps_h[q][:, :], ACT.Gelu)
                    nc.scalar.activation(gh[:, 2 * q:2 * q + 2, :].rearrange("p c n -> p (c n)"), ps_h[q][:, :],
                                         ACT.Gelu).then_inc(gelu_done, 1)
                if not isinstance(n, int) or n + 1 < NTILE:
                    x_hi(n + 1)
                if proj:
                    turned(b, j)
                if conv:
                    a.wait_ge(conv_done, n + 1)
                    if j == 0 and not (isinstance(b, int) and b == 0):
                        a.wait_ge(aocur_done, b)
                    dst = ao_acc[:, :, HG * HD * j:HG * HD * (j + 1)].rearrange("p i (h d) -> p h i d", h=HG)
                    nc.scalar.activation(dst, ps_c.rearrange("p (h i d) -> p h i d", h=HG, d=HD),
                                         ACT.Copy).then_inc(aoevac_done, 1)
                for m in range(2):
                    a.wait_ge(gate_done, n + 1)
                    a.wait_ge(g2_done, 2 * n + m + 1)
                    nc.scalar.activation(yt[:, m, :], ps_y[m][:, D:2 * D], ACT.Copy,
                                         scale=gate[:, m:m + 1]).then_inc(ylo_done, 1)

            def turned(b, j):
                a.wait_ge(aotp_done, NJ * (b - 1) + j + 1)
                nc.scalar.activation(aoT[:, :, ::-1], ps_ot.rearrange("p (k n) -> p k n", k=KD),
                                     ACT.Copy).then_inc(aoT_done, 1)

            a.wait_ge(wo_in, 32)
            for b in range(B - 1):
                a.wait_ge(v_out[b], 16)
            x_hi(0)
            for_tiles(a, tile)
            turned(B, NJ - 1)

        @block.tensor
        def _(pe):
            def turn(t):
                pe.wait_ge(xn_done, t + 1)
                if t >= 2:
                    pe.wait_ge(xnT_done, t - 1)
                for k in range(KD):
                    ins = nc.tensor.transpose(ps_t[t % 2][:, k * P:(k + 1) * P],
                                              xw[:, t, k * P:(k + 1) * P], ident)
                ins.then_inc(tp_done, 1)

            def z_turn(b):
                pe.wait_ge(lg_done, NJ * (b + 1))
                if b >= 1:
                    pe.wait_ge(zexp_done, b)
                for j in range(NJ):
                    ins = nc.tensor.transpose(psz[0:NH, j // 4, (j % 4) * P:(j % 4 + 1) * P],
                                              lg[:, NJ * b + j, NE:NE + NH], ident)
                ins.then_inc(ztp_done, 1)

            pe.wait_ge(const_in, 32)
            pe.wait_ge(w_in, 48)
            turn(0)
            for t in range(NT):
                if t + 1 < NT:
                    turn(t + 1)
                pe.wait_ge(xnT_done, t + 1)
                if t >= 2:
                    pe.wait_ge(post_done, t - 1)
                for k in range(KD):
                    ins = nc.tensor.matmul(ps_p[t % 2][:, 0:NP], xnT[:, t % 2, k, :], wcat[:, k, :],
                                           start=(k == 0), stop=(k == KD - 1))
                ins.then_inc(proj_done, 1)
                if t % NJ == 0 and t > 0:
                    z_turn(t // NJ - 1)
            z_turn(B - 1)

            pe.wait_ge(mask_done, 1)
            mask = maskb[:, :, :].rearrange("p t e -> p (t e)")
            nc.tensor.matmul(ps_rank, cb[:, C_UT:C_UT + P], mask, start=True, stop=False, skip_group_check=True)
            for s in range(1, NT):
                nc.tensor.matmul(ps_rank[:, s * NE:NT * NE], cb[:, C_ONE:C_ONE + P], mask[:, 0:(NT - s) * NE],
                                 start=False, stop=(s == NT - 1), skip_group_check=True)
            nc.tensor.matmul(ps_cnt, cb[:, C_ONE:C_ONE + P], msum[:, :], start=True, stop=True).then_inc(cnt_done, 1)
            for u in range(2 * NT // NB_E):
                pe.wait_ge(onehots, u + 1)
                for i in range(NB_E):
                    s = NB_E * (u % 2) + i
                    ins = nc.tensor.matmul(ps_list, ohr[:, s, :], oha[:, s].rearrange("p v c -> p (v c)"),
                                           start=(u == 0 and i == 0), stop=(NB_E * u + i == 2 * NT - 1),
                                           skip_group_check=True)
                ins.then_inc(listmm_done, 1)

            def x_turn(n, s, k):
                pe.wait_ge(g_in[s], 32 * k + 32)
                if not (isinstance(n, int) and n == 0):
                    pe.wait_ge(xlo_done, n)
                for k in range(KD):
                    for m in range(2):
                        ins = nc.tensor.transpose(ps_x[:, k * TS + m * P:k * TS + (m + 1) * P],
                                                  xs[:, s, m, k * P:(k + 1) * P], ident)
                ins.then_inc(xtp_done, 1)

            def convolve(n, b, j):
                pe.wait_ge(T_in[j % 2], 16 * (NJ // 2 * b + j // 2) + 16)
                if j == 0 and not (isinstance(b, int) and b == 0):
                    pe.wait_ge(v_in, 16 * b)
                if not (isinstance(n, int) and n == 0):
                    pe.wait_ge(aoevac_done, n)
                for h in range(HG):
                    for k in range(NJ):
                        for tl, vl in ((0, 0), (0, 1), (1, 0)):
                            v = vb[0][:, vl, HG * j + h, 0:NJ - k, :]
                            ins = nc.tensor.matmul(ps_c[:, h * P + k * HD:(h + 1) * P],
                                                   tz[:, j % 2, h, tl, (NJ - 1 - k) * P:(NJ - k) * P],
                                                   v.rearrange("p j d -> p (j d)"),
                                                   start=(k == 0 and tl + vl == 0),
                                                   stop=(k == NJ - 1 and tl == 1), skip_group_check=True)
                ins.then_inc(conv_done, 1)

            def turn_out(b, j):
                if j == 0:
                    pe.wait_ge(aocur_done, b)
                else:
                    pe.wait_ge(at_done, NJ * (b - 1) + j)
                for c in range(KD):
                    ins = nc.tensor.transpose(ps_ot[:, c * P:(c + 1) * P], ao[:, j, c * P:(c + 1) * P], ident)
                ins.then_inc(aotp_done, 1)

            def project_out(b, j):
                pe.wait_ge(aoT_done, NJ * (b - 1) + j + 1)
                for c in range(KD):
                    ins = nc.tensor.matmul(ps_o, aoT[:, c, :], wo[:, c, :], start=(c == 0), stop=(c == KD - 1))
                ins.then_inc(wo_done, 1)

            def tile(n, b, j, conv, proj):
                e = pe.value_load(tei[0:1, bass.ds(n, 1)], min_val=0, max_val=NE - 1)
                pe.wait_ge(xlo_done, n + 1)
                for q in range(4):
                    if q == 3:
                        pe.wait_ge(gelu_done, 4 * n + 1)
                    elif not (isinstance(n, int) and n == 0):
                        pe.wait_ge(gelu_done, 4 * n if q == 0 else 4 * n + q - 3)
                    for c in (2 * q, 2 * q + 1):
                        o = ps_h[q][:, (c % 2) * TS:(c % 2 + 1) * TS]
                        for k in range(KD):
                            for wl, xl in ((0, 0), (0, 1), (1, 0)):
                                ins = nc.tensor.matmul(o, w1s[:, e, wl, k, c * P:(c + 1) * P], xT[:, xl, k, :],
                                                       start=(k == 0 and wl + xl == 0),
                                                       stop=(k == KD - 1 and wl == 1))
                    ins.then_inc(g1_done, 1)
                if not isinstance(n, int) or n + 1 < NTILE:
                    x_turn(n + 1, (j + 1) % 2, (NJ // 2) * b + (j + 1) // 2)
                if proj:
                    turn_out(b, j)
                if conv:
                    convolve(n, b, j)
                if proj:
                    project_out(b, j)
                for m in range(2):
                    if not (isinstance(n, int) and n == 0):
                        pe.wait_ge(y_done, 2 * n + m - 1)
                    for c in range(KH):
                        if m == 0 and c % 2 == 0:
                            pe.wait_ge(glo_done, 4 * n + c // 2 + 1)
                        nc.tensor.matmul(ps_y[m], gh[:, c, m * P:(m + 1) * P], w2s[:, e, c, :],
                                         start=(c == 0), stop=False, skip_group_check=True)
                        ins = nc.tensor.matmul(ps_y[m][:, 0:D], gl[:, c, m * P:(m + 1) * P], w2s[:, e, c, 0:D],
                                               start=False, stop=(c == KH - 1), skip_group_check=True)
                    ins.then_inc(g2_done, 1)

            wait_lo(pe, NPIECE - 1)
            wait_lo(pe, LATE0 - 1)
            pe.wait_ge(list_done, 1)
            pe.wait_ge(zexp_done, B)
            pe.wait_ge(post_done, NT)
            pe.wait_ge(wo_in, 32)
            x_turn(0, 0, 0)
            for_tiles(pe, tile)
            turn_out(B, NJ - 1)
            project_out(B, NJ - 1)

        @block.vector
        def _(v):
            def stats(t):
                if t % NJ == 0:
                    v.wait_ge(x_in[t // NJ], 16)
                nc.vector.bn_stats(st[:, t % NJ, :], xw[:, t, :]).then_inc(stats_done, 1)
                v.wait_ge(stats_done, t + 1)
                nc.vector.bn_aggr(mv[:, t, :], st[:, t % NJ, :]).then_inc(aggr_done, 1)

            def norm(t):
                b = t // NJ
                if t % NJ == 0:
                    v.wait_ge(std_done, b + 1)
                    nc.vector.reciprocal(rstd[:, t:t + NJ], std[:, t:t + NJ]).then_inc(rstd_done, 1)
                    v.wait_ge(rstd_done, b + 1)
                nc.vector.tensor_scalar(xw[:, t, :], xw[:, t, :], mv[:, t, 0:1], rstd[:, t:t + 1],
                                        ALU.subtract, ALU.mult).then_inc(xn_done, 1)

            def post(t):
                slot = vb[V_SLOT[t // NJ]]
                v.wait_ge(vhi_done, t + 1)
                nc.vector.tensor_copy(lg[:, t, :], ps_p[t % 2][:, 0:NE + NH]).then_inc(lg_done, 1)
                nc.vector.tensor_tensor(slot[:, 1, :, t % NJ, :],
                                        ps_p[t % 2][:, NE + NH:NP].rearrange("p (h d) -> p h d", h=NH),
                                        slot[:, 0, :, t % NJ, :], ALU.subtract).then_inc(post_done, 1)

            def z_max(b):
                v.wait_ge(ztp_done, b + 1)
                nc.vector.tensor_reduce(zst[:, 0:1], psz[0:NH, :, :].rearrange("p a n -> p (a n)"), AX.X,
                                        ALU.max).then_inc(zmax_done, 1)
                v.wait_ge(zmax_done, b + 1)
                nc.vector.tensor_scalar(zst[:, 1:2], zst[:, 0:1], -SCALE, None, ALU.mult).then_inc(zneg_done, 1)

            def z_scale(b):
                v.wait_ge(zexp_done, b + 1)
                nc.vector.reciprocal(zst[:, 3:4], zst[:, 2:3]).then_inc(zrec_done, 1)
                v.wait_ge(zrec_done, b + 1)
                nc.vector.tensor_scalar(ez[:, :], ez[:, :], zst[:, 3:4], None, ALU.mult).then_inc(zn_done, 1)

            def z_low(b):
                v.wait_ge(zhi_done, b + 1)
                if b == 0:
                    v.wait_ge(zpad_done, 1)
                nc.vector.tensor_tensor(zhl[:, 1, 0:S], ez[:, :], zhl[:, 0, 0:S],
                                        ALU.subtract).then_inc(zsplit_done, 1)

            nc.vector.memset(eps[:, :], EPS).then_inc(eps_done, 1)
            for t in range(NJ):
                stats(t)
            for t in range(NJ):
                norm(t)
            for t in range(NJ, 2 * NJ):
                stats(t)
            for t in range(NT):
                b, j = t // NJ, t % NJ
                post(t)
                if b + 1 < B:
                    norm(t + NJ)
                if b + 2 < B:
                    stats(t + 2 * NJ)
                if b >= 1:
                    if j == 1:
                        z_max(b - 1)
                    if j == 4:
                        z_scale(b - 1)
                    if j == 6:
                        z_low(b - 1)
                c = piece_at(t - 1) if t else None
                if c is not None and on_dve(c):
                    hi, lo, s, _src = w_piece(c)
                    v.wait_ge(whi_done, c + 1)
                    nc.vector.tensor_tensor(lo, s, hi, ALU.subtract).then_inc(wdve_done, 1)
            z_max(B - 1)

            done = [0]

            def step(ins):
                done[0] += 1
                ins.then_inc(route, 1)
                v.wait_ge(route, done[0])

            def wide(col):
                return col.unsqueeze(2).to_broadcast([P, NT, NE])

            v.wait_ge(const_in, 32)
            v.wait_ge(lg_done, NT)
            c = [c32[:, i, :] for i in range(4)]
            step(nc.vector.tensor_reduce(c[0], lg[:, :, 0:NE], AX.X, ALU.max))
            nc.vector.tensor_tensor(prob[:, :, :], lg[:, :, 0:NE], wide(c[0]), ALU.subtract).then_inc(rsub_done, 1)
            v.wait_ge(route_exp, 1)
            step(nc.vector.tensor_reduce(c[1], prob[:, :, :], AX.X, ALU.add))
            step(nc.vector.reciprocal(c[2], c[1]))
            step(nc.vector.tensor_tensor(prob[:, :, :], prob[:, :, :], wide(c[2]), ALU.mult))
            ew = cf[:, C_EW:C_EW + NE].unsqueeze(1).to_broadcast([P, NT, NE])
            left = prob
            for oh in (oh1, oh2):
                step(nc.vector.tensor_reduce(c[0], left[:, :, :], AX.X, ALU.max))
                step(nc.vector.tensor_tensor(oh[:, :, :], left[:, :, :], wide(c[0]), ALU.is_equal))
                step(nc.vector.tensor_tensor(oh[:, :, :], oh[:, :, :], ew, ALU.mult))
                step(nc.vector.tensor_reduce(c[1], oh[:, :, :], AX.X, ALU.max))
                step(nc.vector.tensor_tensor(oh[:, :, :], oh[:, :, :], wide(c[1]), ALU.is_equal))
                if oh is oh1:
                    step(nc.vector.scalar_tensor_tensor(t8[:, :, :], oh1[:, :, :], -2.0, prob[:, :, :],
                                                        ALU.mult, ALU.add))
                    left = t8
            step(nc.vector.tensor_tensor(rank[:, :, :], oh1[:, :, :], oh2[:, :, :], ALU.add))
            step(nc.vector.tensor_copy(maskb[:, :, :], rank[:, :, :]))
            with nc.allow_low_precision("sums of at most 32 ones are exact"):
                step(nc.vector.tensor_reduce(msum[:, :], rank[:, :, :].rearrange("p t e -> p e t"), AX.X, ALU.add))
            nc.vector.tensor_tensor(t8[:, :, :], rank[:, :, :], prob[:, :, :], ALU.mult).then_inc(mask_done, 1)
            z_scale(B - 1)

            v.wait_ge(cnt_done, 1)
            e = [e8[:, i, :] for i in range(6)]
            step(nc.vector.tensor_scalar(e8i[:, 0, :], ps_cnt, float(TS - 1), None, ALU.add))
            step(nc.vector.tensor_scalar(e8i[:, 1, :], e8i[:, 0, :], 8, None, ALU.arith_shift_right))
            step(nc.vector.tensor_copy(e[0], e8i[:, 1, :]))
            step(nc.vector.memset(e[1], 1.0))
            step(nc.vector.tensor_tensor_scan(e[2], e[1], e[0], 0.0, ALU.mult, ALU.add))
            step(nc.vector.tensor_tensor(e[3], e[2], e[0], ALU.subtract))
            step(nc.vector.tensor_scalar(e[4], e[3], float(TS), None, ALU.mult))
            step(nc.vector.tensor_tensor(rank[:, :, :], ps_rank.rearrange("p (t e) -> p t e", e=NE),
                                         e[4].unsqueeze(1).to_broadcast([P, NT, NE]), ALU.add))
            for i, oh in enumerate((oh1, oh2)):
                step(nc.vector.tensor_tensor(oh[:, :, :], oh[:, :, :], rank[:, :, :], ALU.mult))
                step(nc.vector.tensor_reduce(posf[:, :, i], oh[:, :, :], AX.X, ALU.add))
            pf, pi = (z[:, :, :].rearrange("p t a -> p (t a)") for z in (posf, posi))
            step(nc.vector.tensor_copy(pi, pf))
            step(nc.vector.tensor_scalar(pi, pi, 7, None, ALU.arith_shift_right))
            step(nc.vector.tensor_copy(colA[:, :], pi))
            step(nc.vector.scalar_tensor_tensor(colR[:, :], colA[:, :], -float(P), pf, ALU.mult, ALU.add))
            z_low(B - 1)

            def one_hots(u):
                if u >= 2:
                    v.wait_ge(listmm_done, u - 1)
                k, s = NB_E * u, NB_E * (u % 2)
                nc.vector.tensor_tensor(ohe[:, s:s + NB_E, :],
                                        cb[:, C_IA:C_IA + NCOL].unsqueeze(1).to_broadcast([P, NB_E, NCOL]),
                                        colA[:, k:k + NB_E].unsqueeze(2).to_broadcast([P, NB_E, NCOL]),
                                        ALU.is_equal)
                nc.vector.tensor_tensor(ohr[:, s:s + NB_E, :],
                                        cb[:, C_IR:C_IR + P].unsqueeze(1).to_broadcast([P, NB_E, P]),
                                        colR[:, k:k + NB_E].unsqueeze(2).to_broadcast([P, NB_E, P]),
                                        ALU.is_equal).then_inc(oneh_done, 1)

            v.wait_ge(zsplit_done, B)
            for u in range(2 * NT // NB_E):
                one_hots(u)
            step(nc.vector.memset(ge9[:, :, 0:1], 1.0))
            step(nc.vector.memset(ge9[:, :, NE:NE + 1], 0.0))
            step(nc.vector.tensor_tensor(
                ge9[:, :, 1:NE], cf[:, C_S:C_S + NTILE].unsqueeze(2).to_broadcast([P, NTILE, NE - 1]),
                e8[:, 2, 0:NE - 1].unsqueeze(1).to_broadcast([P, NTILE, NE - 1]), ALU.is_ge))
            step(nc.vector.tensor_tensor(teoh[:, :, :], ge9[:, :, 0:NE], ge9[:, :, 1:NE + 1], ALU.subtract))
            step(nc.vector.tensor_reduce(tef[:, :], ge9[:, :, 1:NE], AX.X, ALU.add))
            step(nc.vector.tensor_copy(tei[:, :], tef[:, :]))
            v.wait_ge(listmm_done, 2 * NT // NB_E)
            step(nc.vector.tensor_copy(idf[:, :, :].rearrange("p v c -> p (v c)"), ps_list))
            step(nc.vector.scalar_tensor_tensor(idf[:, 1, :], idf[:, 0, :], float(P), idf[:, 1, :],
                                                ALU.mult, ALU.add))
            step(nc.vector.tensor_scalar(idf[:, 0, :], idf[:, 0, :], 0.0, None, ALU.is_equal))
            step(nc.vector.tensor_tensor(idf[:, 0, :], idf[:, 0, :], cf[:, C_PAD:C_PAD + NCOL], ALU.mult))
            step(nc.vector.tensor_tensor(idf[:, 1, :], idf[:, 1, :], idf[:, 0, :], ALU.add))
            nc.vector.tensor_scalar(idt[:, :], idf[:, 1, :], -float(P), None, ALU.add).then_inc(list_done, 1)

            def x_lo(n):
                v.wait_ge(xhi_done, n + 1)
                nc.vector.tensor_tensor(xT[:, 1].rearrange("p k n -> p (k n)"), ps_x[:, :],
                                        xT[:, 0].rearrange("p k n -> p (k n)"), ALU.subtract).then_inc(xlo_done, 1)

            def gates(n, s, k):
                v.wait_ge(g_in[s], 32 * k + 32)
                nc.vector.tensor_tensor(g8[:, :, :], xs[:, s, :, D:ROW],
                                        teoh[:, bass.ds(n, 1), :].to_broadcast([P, 2, NE]),
                                        ALU.mult).then_inc(g8_done, 1)
                v.wait_ge(g8_done, n + 1)
                nc.vector.tensor_reduce(gate[:, :], g8[:, :, :], AX.X, ALU.add).then_inc(gate_done, 1)

            def rows(b, j):
                v.wait_ge(wo_done, NJ * (b - 1) + j + 1)
                nc.vector.tensor_tensor(at[:, j % 4, :], ps_o, bo[:, :], ALU.add).then_inc(at_done, 1)

            def tile(n, b, j, conv, proj):
                if j == 0 and proj:
                    v.wait_ge(aoevac_done, n)
                    nc.vector.tensor_copy(ao[:, :, :], ao_acc[:, :, :]).then_inc(aocur_done, 1)
                for q in range(4):
                    v.wait_ge(gelu_done, 4 * n + q + 1)
                    nc.vector.tensor_tensor(gl[:, 2 * q:2 * q + 2, :].rearrange("p c n -> p (c n)"),
                                            act[:, q % 2, :],
                                            gh[:, 2 * q:2 * q + 2, :].rearrange("p c n -> p (c n)"),
                                            ALU.subtract).then_inc(glo_done, 1)
                more = not isinstance(n, int) or n + 1 < NTILE
                if more:
                    x_lo(n + 1)
                if proj:
                    rows(b, j)
                for m in range(2):
                    v.wait_ge(ylo_done, 2 * n + m + 1)
                    if not (isinstance(n, int) and n == 0):
                        landed = acc_before(n - 1, b, j - 1) + 1 if j else acc_before(n, b, 0) - 1
                        v.wait_ge(acc_out, 16 * (landed + m))
                    nc.vector.scalar_tensor_tensor(y[:, m, :], ps_y[m][:, 0:D], gate[:, m:m + 1], yt[:, m, :],
                                                   ALU.mult, ALU.add).then_inc(y_done, 1)
                if more:
                    gates(n + 1, (j + 1) % 2, (NJ // 2) * b + (j + 1) // 2)

            v.wait_ge(wo_in, 32)
            x_lo(0)
            gates(0, 0, 0)
            for_tiles(v, tile)
            rows(B, NJ - 1)


def kernel(**inputs):
    import numpy as np
    import ml_dtypes
    import concourse.bacc as bacc
    from concourse import mybir as mb
    from concourse.bass_utils import run_bass_kernel_spmd as run

    cf = np.zeros((P, C_F), np.float32)
    cf[:, C_ID:C_ID + P] = np.eye(P)
    cf[:, C_P] = np.arange(P)
    cf[:, C_EW:C_EW + NE] = NE - np.arange(NE)
    cf[:, C_S:C_S + NTILE] = np.arange(NTILE)
    cf[:, C_PAD:C_PAD + NCOL] = P + TOK + (np.arange(NCOL) % 2)[None, :] * P + np.arange(P)[:, None]
    cb = np.zeros((P, C_B), np.float32)
    cb[:, C_UT:C_UT + P] = np.triu(np.ones((P, P)), 1)
    cb[:, C_ONE:C_ONE + P] = 1
    cb[:, C_IR:C_IR + P] = np.arange(P)
    cb[:, C_IA:C_IA + NCOL] = np.arange(NCOL)
    cb = cb.astype(ml_dtypes.bfloat16)

    def laid(a, *order):
        a = np.asarray(a)
        return np.ascontiguousarray(a.transpose(order) if order else a)

    arrays = {
        "x": laid(inputs["L0_attn_x"]).reshape(TOK, D),
        "routerT": laid(inputs["L0_ffn_router_w"], 1, 0),
        "waT": laid(inputs["L0_attn_W_A"], 1, 0),
        "wvT": laid(inputs["L0_attn_W_V"], 1, 0),
        "woT": laid(inputs["L0_attn_W_O"], 1, 0),
        "b_o": laid(inputs["L0_attn_b_O"]),
        "w1T": laid(inputs["L0_ffn_w1"], 0, 2, 1),
        "w2T": laid(inputs["L0_ffn_w2"], 0, 2, 1),
        "const_f": cf,
        "const_b": cb,
        "zeros": np.zeros((PADROWS, ROW), np.float32),
    }
    nc = bacc.Bacc("TRN2", target_bir_lowering=False, num_devices=1)
    args = [nc.dram_tensor(n, a.shape, mb.dt.from_np(a.dtype), kind="ExternalInput").ap() for n, a in arrays.items()]
    args.append(nc.dram_tensor("out", (TOK + PADROWS, D), F32, kind="ExternalOutput").ap())
    build(nc, *args)
    r = run(nc, [arrays], core_ids=[0])
    return r.results[0]["out"][0:TOK].reshape(B, S, D)
```

```python
from contextlib import ExitStack

import concourse.bass as bass
from concourse import mybir

F32 = mybir.dt.float32
BF16 = mybir.dt.bfloat16
I32 = mybir.dt.int32
U32 = mybir.dt.uint32
ALU = mybir.AluOpType
ACT = mybir.ActivationFunctionType
AX = mybir.AxisListType

P = 128
B, S, D = 4, 1024, 256
NH, HD = 16, 16
NE, H = 8, 1024
TOK = B * S
NT = TOK // P
NJ = S // P
KD = D // P
KH = H // P
NP = NE + NH + D
TS = 256
NTILE = (2 * TOK) // TS + NE - 1
NCOL = NTILE * TS // P
ROW = D + NE
PADROWS = 2 * P
NZ = S + P
HG = NH // NJ
NU = B * NJ
LEAD = 3
SH = 6
MAYBE = NU + NJ - SH
LN = ((0, 4), (4, 8), (8, 16), (16, 24), (24, 32))
NPS = 4
LATE0 = 24
PIECE = 1024
NPIECE = NE * 2 * KD * H // PIECE
NSTG = 4
NB_E = 8
SCALE = float(HD) ** -0.5
EPS = 1e-5

C_ID, C_P, C_EW, C_S, C_PAD = 0, 128, 129, 137, 137 + NTILE
C_F = C_PAD + NCOL
C_UT, C_ONE, C_IR, C_IA = 0, 128, 256, 384
C_B = C_IA + NCOL


def build(nc, x, routerT, waT, wvT, woT, b_o, w1T, w2T, const_f, const_b, zeros, out):
    x_b = x.rearrange("(b t p) d -> b p t d", p=P, t=NJ)
    x_cp = x.rearrange("(b a r) d -> b a (r d)", a=P, b=B)
    out_b = out[0:TOK, :].rearrange("(b a r) d -> b a (r d)", a=P, b=B)
    out_pair = out[0:TOK, :].rearrange("(g t p) d -> g p t d", p=P, t=2)
    w1_v = w1T.rearrange("e (k p) h -> e k p h", p=P)
    w2_v = w2T.rearrange("e (f c p) d -> e f p c d", p=P, f=2)

    with ExitStack() as ctx:
        xn_dram = nc.dram_tensor("xn_table", [TOK + PADROWS, ROW], F32).ap()
        z_dram = nc.dram_tensor("z_reversed", [B, NJ, HG, 2, NZ], BF16).ap()
        v_dram = nc.dram_tensor("v_halves", [B, P, 2 * NH * NJ * HD], BF16).ap()
        xn_rows = xn_dram[0:TOK, :].rearrange("(b t p) d -> b p t d", p=P, t=NJ)
        xn_w8 = xn_dram[0:TOK, :].rearrange("(t p) d -> p t d", p=P)

        cursor = [16512]

        def sb(name, shape, dt, zone=None):
            size = 4 if dt in (F32, I32, U32) else 2
            for n in shape[1:]:
                size *= n
            c = cursor if zone is None else zone
            t = nc.alloc_sbuf_tensor_at(name, shape, dt, offset=c[0])
            c[0] += (size + 31) // 32 * 32
            return t

        w1s = sb("w1s", [P, NE, 2, KD, H], BF16)
        w2_at = cursor[0]
        w2s = sb("w2s", [P, NE, KH, 2 * D], BF16)
        zone = [w2_at + 4 * KH * 2 * D * 2]
        xw = sb("x_normed", [P, NT, D], F32, zone)
        assert zone[0] == cursor[0]

        zone = [cursor[0]]
        stage = sb("w_stage", [P, NSTG, PIECE], F32)
        tz = sb("toeplitz", [P, 2, HG, 2, S], BF16, zone)
        assert zone[0] == cursor[0]

        zone = [cursor[0]]
        vb = [sb(f"v_split{i}", [P, 2, NH, NJ, HD], BF16, zone) for i in range(3)]
        cursor[0] += 2 * NH * NJ * HD * 2
        ao_acc = sb("attn_conv", [P, NJ, D], F32)
        ao = sb("attn_out", [P, NJ, D], F32)
        assert zone[0] == cursor[0]

        zone = [cursor[0]]
        ez = sb("z_exp", [NH, S], F32, zone)
        zhl = sb("z_split", [NH, 2, NZ], BF16, zone)
        z_end = zone[0]
        ohr = nc.alloc_sbuf_tensor_at("onehot_r", [P, 2 * NB_E, P], BF16, offset=zone[0])
        xnT = sb("xnT", [P, 2, KD, P], F32, zone)
        wcat = sb("w_cat", [P, KD, NP], F32, zone)
        lg = sb("logits", [P, NT, NE + NH], F32, zone)
        prob = sb("prob", [P, NT, NE], F32, zone)
        t8 = sb("route_t8", [P, NT, NE], F32, zone)
        oh1 = sb("onehot1", [P, NT, NE], F32, zone)
        oh2 = sb("onehot2", [P, NT, NE], F32, zone)
        rank = sb("rank", [P, NT, NE], F32, zone)
        maskb = sb("mask_bf", [P, NT, NE], BF16, zone)
        c32 = sb("cols32", [P, 4, NT], F32, zone)
        posf = sb("pos_f", [P, NT, 2], F32, zone)
        posi = sb("pos_i", [P, NT, 2], I32, zone)
        first = sb("not_first_tile", [P, NE, NT], BF16, zone)
        prefix = sb("mask_prefix", [P, NE, NT], BF16, zone)
        ohe = sb("onehot_a", [P, 2 * NB_E, NCOL], BF16, zone)
        oha = sb("onehot_tp", [P, 2 * NB_E, 2, NCOL], BF16, zone)
        ge9 = sb("tile_ge", [P, NTILE, NE + 1], F32, zone)
        idf = sb("list_f", [P, 2, NCOL], F32, zone)
        front_end = zone[0]
        zone = [cursor[0]]
        at = sb("attn_rows", [P, 4, D], F32, zone)
        yt = sb("y_lo", [P, 2, D], F32, zone)
        y = sb("y", [P, 2, D], F32, zone)
        bo = sb("b_o", [P, D], F32, zone)
        assert zone[0] >= z_end
        xs = sb("x_sorted", [P, 2, 2, ROW], F32, zone)
        xT = sb("xT_split", [P, 2, KD, TS], BF16, zone)
        act = sb("gelu", [P, 2, 2 * TS], F32, zone)
        gh = sb("gelu_hi", [P, KH, TS], BF16, zone)
        gl = sb("gelu_lo", [P, KH, TS], BF16, zone)
        wo = sb("w_o", [P, KD, D], F32, zone)
        cursor[0] = max(front_end, zone[0])

        aoT = sb("attn_outT", [P, KD, P], F32)
        cf = sb("const_f", [P, C_F], F32)
        cb = sb("const_b", [P, C_B], BF16)
        st = sb("stats", [P, NJ, 6], F32)
        mv = sb("mean_var", [P, NT, 2], F32)
        std = sb("std", [P, NT], F32)
        rstd = sb("rstd", [P, NT], F32)
        zst = sb("z_stats", [NH, 4], F32)
        eps = sb("eps", [P, 1], F32)
        warm = sb("warm", [P, 1], F32)
        colA = sb("place_col", [P, 2 * NT], F32)
        colR = sb("place_row", [P, 2 * NT], F32)
        e8 = sb("per_expert", [P, 6, NE], F32)
        e8i = sb("per_expert_i", [P, 2, NE], I32)
        teoh = sb("tile_onehot", [P, NTILE, NE], F32)
        tef = sb("tile_expert_f", [P, NTILE], F32)
        tei = sb("tile_expert", [P, NTILE + 1], I32)
        idt = sb("list", [P, NCOL], U32)
        idxs = sb("gather_index", [P, 4, 2], U32)
        g8 = sb("gate8", [P, 2, NE], F32)
        gate = sb("gate", [P, 2], F32)
        held = sb("held", [P, 5], F32)
        assert cursor[0] <= nc.sbuf_usable_end, cursor[0]

        bank = [ctx.enter_context(nc.psum_tensor(f"bank{i}", [P, 512], F32)) for i in range(4)]
        psz = ctx.enter_context(nc.psum_tensor("bank45", [P, 2, 512], F32))
        bank6 = ctx.enter_context(nc.psum_tensor("bank6", [P, 512], F32))
        bank7 = ctx.enter_context(nc.psum_tensor("bank7", [P, 512], F32))
        ps_t, ps_p = bank[0:2], (bank[2], bank[3], bank6, bank7)
        ps_rank = bank6[:, 0:NT * NE]
        ps_cnt = bank7[:, 256:256 + NE]
        ps_list = bank7[:, 0:2 * NCOL]
        ps_h = [bank[0], bank[1], bank[2], bank[0]]
        ps_c = bank[3][:, 0:HG * P]
        ps_y = [psz[:, 0, :], psz[:, 1, :]]
        ps_x = bank6
        ps_ot, ps_o = bank7[:, 0:D], bank7[:, D:2 * D]

        ident = cf[:, C_ID:C_ID + P]

        def sems(text):
            return [ctx.enter_context(nc.semaphore(n)) for n in text.split()]

        const_in, w_in, wo_in, pads_out, x_out, xn_out, z_out, w8_out = sems(
            "const_in w_in wo_in pads_out x_out xn_out z_out w8_out")
        x_in = sems("x_in0 x_in1 x_in2 x_in3 x_in0b")
        stage_in = sems("stage_in0 stage_in1 stage_in2 stage_in3")
        T_in = sems("T_in0 T_in1")
        g_in = sems("g_in0 g_in1")
        v_out = sems("v_out1 v_out2 v_out3")
        v_in, acc_out = sems("v_in acc_out")
        eps_done, zpad_done, held_done, stats_done, aggr_done, std_done, rstd_done, xn_done = sems(
            "eps_done zpad_done held_done stats_done aggr_done std_done rstd_done xn_done")
        tp_done, xnT_done, proj_done, lg_done, vhi_done, post_done, whi_done, wlo_done = sems(
            "tp_done xnT_done proj_done lg_done vhi_done post_done whi_done wlo_done")
        ztp_done, zmax_done, zneg_done, zexp_done, zrec_done, zhi_done, zsplit_done = sems(
            "ztp_done zmax_done zneg_done zexp_done zrec_done zhi_done zsplit_done")
        (route, route_exp, rsub_done, mask_done, gates_done, cnt_done, oneh_done,
         rows_done, first_done, tile_part, row_part, listmm_done, list_done, tiles_done) = sems(
            "route route_exp rsub_done mask_done gates_done cnt_done oneh_done "
            "rows_done first_done tile_part row_part listmm_done list_done tiles_done")
        idx_done, xtp_done, xhi_done, xlo_done, g1_done, gelu_done, glo_done, g2_done, ylo_done, y_done = sems(
            "idx_done xtp_done xhi_done xlo_done g1_done gelu_done glo_done g2_done ylo_done y_done")
        g8_done, gate_done, conv_done, aoevac_done, aocur_done, aotp_done, aoT_done, wo_done, at_done = sems(
            "g8_done gate_done conv_done aoevac_done aocur_done aotp_done aoT_done wo_done at_done")
        V_SLOT = (0, 1, 2, 1)

        def w_piece(c):
            m, e, f = c // (NPIECE // 2), c % (NPIECE // 2) // 2, c % 2
            s = stage[:, c % NSTG, :]
            if m == 0:
                return w1s[:, e, 0, f], w1s[:, e, 1, f], s, w1_v[e, f]
            half = w2s[:, e, f * KH // 2:(f + 1) * KH // 2]
            return half[:, :, 0:D], half[:, :, D:2 * D], s.rearrange("p (c d) -> p c d", d=D), w2_v[e, f]

        def load_piece(eng, c):
            if c >= NSTG:
                eng.wait_ge(wlo_done, c - NSTG + 1)
            _hi, _lo, s, src = w_piece(c)
            eng.dma_start(s, src).then_inc(stage_in[c % NSTG], 16)

        def piece_at(t):
            return 3 * (t // 4) + t % 4 if t % 4 < 3 else None

        def acc_before(n, b, j):
            if isinstance(n, int):
                return 2 * n + min(max(n - NJ + SH, 0), NU) // 2
            return 20 * b + 2 * j + (j - NJ + SH) // 2

        def for_tiles(eng, run):
            def units(n, b, j):
                conv = (b, j + SH) if j + SH < NJ else (b + 1, j + SH - NJ)
                proj = (conv[0] - 1, conv[1])
                if isinstance(n, int):
                    conv, proj = conv if n + SH < NU else None, proj if 0 <= n + SH - NJ < NU else None
                run(n, b, j, conv, proj)

            for n in range(NJ):
                units(n, 0, n)
            with eng.Fori(1, B - 1) as b:
                for j in range(NJ):
                    units(NJ * b + j, b, j)
            for n in range(NU - NJ, MAYBE):
                units(n, n // NJ, n % NJ)
            eng.wait_ge(tiles_done, 1)
            used = eng.value_load(tei[0:1, NTILE:NTILE + 1], min_val=2 * TOK // TS, max_val=NTILE)
            for n in range(MAYBE, NTILE):
                with eng.If(used > n):
                    units(n, n // NJ, n % NJ)

        block = ctx.enter_context(nc.Block())

        @block.sync
        def _(sp):
            sp.dma_start(xw[:, 0:NJ // 2, :], x_b[0, :, 0:NJ // 2]).then_inc(x_in[0], 16)
            sp.dma_start(cf[:, :], const_f).then_inc(const_in, 16)
            sp.dma_start(xw[:, NJ // 2:NJ, :], x_b[0, :, NJ // 2:NJ]).then_inc(x_in[4], 16)
            sp.dma_start(wcat[:, :, 0:NE], routerT.rearrange("(k p) n -> p k n", p=P)).then_inc(w_in, 16)
            sp.dma_start(wcat[:, :, NE:NE + NH], waT.rearrange("(k p) n -> p k n", p=P)).then_inc(w_in, 16)
            sp.dma_start(wcat[:, :, NE + NH:NP], wvT.rearrange("(k p) n -> p k n", p=P)).then_inc(w_in, 16)
            load_piece(sp, 0)
            sp.dma_start(xw[:, NJ:2 * NJ, :], x_b[1]).then_inc(x_in[1], 16)
            load_piece(sp, 1)
            sp.dma_start(cb[:, :], const_b).then_inc(const_in, 16)
            sp.dma_start(xw[:, 2 * NJ:3 * NJ, :], x_b[2]).then_inc(x_in[2], 16)
            load_piece(sp, 2)
            sp.dma_start(xw[:, 3 * NJ:4 * NJ, :], x_b[3]).then_inc(x_in[3], 16)
            sp.dma_start(xn_dram[TOK:TOK + PADROWS, :], zeros).then_inc(pads_out, 16)
            sp.dma_start(out[TOK:TOK + PADROWS, :], zeros[:, 0:D]).then_inc(x_out, 16)

            def rows_out(b):
                sp.wait_ge(xn_done, NJ * (b + 1))
                sp.dma_start(xn_rows[b, :, :, 0:D], xw[:, NJ * b:NJ * (b + 1), :]).then_inc(xn_out, 16)

            def z_write(b):
                sp.wait_ge(zsplit_done, b + 1)
                sp.dma_start(z_dram[b].rearrange("u h l s -> (u h) l s"), zhl[:, :, :]).then_inc(z_out, 16)

            def v_write(b):
                sp.wait_ge(post_done, NJ * (b + 1))
                sp.dma_start(v_dram[b], vb[V_SLOT[b]][:, :, :, :, :].rearrange("p l h j d -> p (l h j d)")
                             ).then_inc(v_out[b - 1], 16)

            rows_out(0)
            for b in range(B):
                if b + 1 < B:
                    rows_out(b + 1)
                if b >= 1:
                    z_write(b - 1)
                    if b == 1:
                        v_write(b)
            sp.wait_ge(whi_done, NPIECE - 2)
            v_write(2)
            v_write(3)
            sp.wait_ge(gates_done, 1)
            sp.dma_start(xn_w8[:, :, D:ROW], t8[:, :, :]).then_inc(w8_out, 16)

            def toeplitz(b, j):
                src = z_dram[b, j]
                src = bass.AP(src.tensor, src.offset, [[1, P], [NZ, HG * 2], [1, S]])
                sp.dma_start(tz[:, j % 2].rearrange("p h l s -> p (h l) s"), src).then_inc(T_in[j % 2], 16)

            def x_copy(q):
                sp.dma_start(out_b[q], x_cp[q]).then_inc(x_out, 16)

            def reload(b, j, last):
                sp.wait_ge(conv_done, NJ * b + j + 1)
                if j + 2 < NJ:
                    toeplitz(b, j + 2)
                elif not last:
                    toeplitz(b + 1, j + 2 - NJ)
                if j == NJ - 1 and not last:
                    sp.dma_start(vb[0][:, :, :, :, :].rearrange("p l h j d -> p (l h j d)"),
                                 v_dram[b + 1]).then_inc(v_in, 16)

            sp.wait_ge(wlo_done, NPIECE)
            sp.wait_ge(z_out, 16 * (B - 1))
            toeplitz(0, 0)
            toeplitz(0, 1)
            x_copy(0)
            x_copy(1)
            for j in range(SH - 1):
                reload(0, j, False)
            z_write(B - 1)
            for b in range(B - 1):
                sp.wait_ge(v_out[b], 16)
            sp.wait_ge(list_done, 1)
            sp.wait_ge(z_out, 16 * B)
            sp.dma_start(wo[:, :, :], woT.rearrange("(k p) n -> p k n", p=P)).then_inc(wo_in, 16)
            sp.dma_start(bo[:, :], b_o.partition_broadcast(P)).then_inc(wo_in, 16)
            x_copy(2)
            x_copy(3)
            for j in range(SH - 1, NJ):
                reload(0, j, False)
            with sp.Fori(1, B - 1) as b:
                for j in range(NJ):
                    reload(b, j, False)
            for j in range(NJ - 2):
                reload(B - 1, j, True)

        @block.gpsimd
        def _(pool):
            nc.gpsimd.memset(held[:, :], 0.0).then_inc(held_done, 1)
            nc.gpsimd.memset(zhl[:, :, S:NZ], 0.0).then_inc(zpad_done, 1)
            for c in range(NPIECE):
                hi, lo, s, _src = w_piece(c)
                pool.wait_ge(whi_done, c + 1)
                nc.gpsimd.tensor_tensor(lo, s, hi, ALU.subtract).then_inc(wlo_done, 1)

            def hold(i, n):
                if not isinstance(n, int):
                    nc.gpsimd.tensor_tensor(held[:, i:i + 1], held[:, 4:5], held[:, 4:5], ALU.add)

            def gather(n, s, si):
                nc.gpsimd.tensor_copy(idxs[:, si, :], idt[:, bass.ds(2 * n, 2)]).then_inc(idx_done, 1)
                pool.wait_ge(idx_done, n + 1)
                hold(0, n)
                for m in range(2):
                    nc.gpsimd.indirect_dma_start(
                        out=xs[:, s, m, :], out_offset=None, in_=xn_dram[:, :],
                        in_offset=bass.IndirectOffsetOnAxis(ap=idxs[:, si, m:m + 1], axis=0),
                    ).then_inc(g_in[s], 16)

            def tile(n, b, j, conv, proj):
                before = acc_before(n, b, j)
                if not isinstance(n, int) or n + 2 < NTILE:
                    pool.wait_ge(gate_done, n + 1)
                    pool.wait_ge(xtp_done, n + 1)
                    gather(n + 2, j % 2, (j + 2) % 4)
                for m in range(2):
                    pool.wait_ge(y_done, 2 * n + m + 1)
                    if isinstance(n, int) and n == 0:
                        pool.wait_ge(x_out, 16 * (B + 1))
                    if not (isinstance(n, int) and n == 0 and m == 0):
                        pool.wait_ge(acc_out, 16 * (before + m))
                    hold(1 + m, n)
                    nc.gpsimd.indirect_dma_start(
                        out=out[:, :], out_offset=bass.IndirectOffsetOnAxis(ap=idxs[:, j % 4, m:m + 1], axis=0),
                        in_=y[:, m, :], in_offset=None, compute_op=ALU.add,
                    ).then_inc(acc_out, 16)
                if proj and j % 2 == 1:
                    add_rows(*proj, before + 2)
                if isinstance(n, int) and n >= MAYBE - 1:
                    pool.wait_ge(acc_out, 16 * acc_before(n + 1, 0, 0))

            def add_rows(b, j, before):
                pool.wait_ge(at_done, NJ * b + j + 1)
                pool.wait_ge(acc_out, 16 * before)
                hold(3, b)
                k = (j - 1) % 4
                nc.gpsimd.dma_start(out_pair[(NJ // 2) * b + j // 2], at[:, k:k + 2, :],
                                    accum_op=ALU.add).then_inc(acc_out, 16)

            pool.wait_ge(const_in, 32)
            for u in range(2 * NT // NB_E):
                pool.wait_ge(oneh_done, u + 1)
                if u >= 2:
                    pool.wait_ge(listmm_done, u - 1)
                k = NB_E * (u % 2)
                nc.gpsimd.tensor_tensor(oha[:, k:k + NB_E, 1, :], ohe[:, k:k + NB_E, :],
                                        cf[:, C_P:C_P + 1].unsqueeze(2).to_broadcast([P, NB_E, NCOL]),
                                        ALU.mult).then_inc(row_part, 1)
            pool.wait_ge(held_done, 1)
            pool.wait_ge(list_done, 1)
            pool.wait_ge(xn_out, 16 * B)
            pool.wait_ge(w8_out, 16)
            pool.wait_ge(pads_out, 16)
            gather(0, 0, 0)
            gather(1, 1, 1)
            for_tiles(pool, tile)

        @block.scalar
        def _(a):
            def split_hi(c):
                hi, _lo, s, _src = w_piece(c)
                a.wait_ge(stage_in[c % NSTG], 16 * (c // NSTG + 1))
                nc.scalar.activation(hi, s, ACT.Copy).then_inc(whi_done, 1)

            def std_of(g):
                lo, hi = LN[g]
                a.wait_ge(aggr_done, hi)
                nc.scalar.activation(std[:, lo:hi], mv[:, lo:hi, 1], ACT.Sqrt,
                                     bias=eps[:, :]).then_inc(std_done, 1)

            def turned_in(t):
                a.wait_ge(tp_done, t + 1)
                if t >= 2:
                    a.wait_ge(proj_done, t - 1)
                nc.scalar.activation(xnT[:, t % 2].rearrange("p k n -> p (k n)"), ps_t[t % 2][:, 0:D],
                                     ACT.Copy).then_inc(xnT_done, 1)

            def z_exp(b):
                a.wait_ge(zneg_done, b + 1)
                if b >= 1:
                    a.wait_ge(zsplit_done, b)
                nc.scalar.activation(ez[:, ::-1], psz[0:NH, :, :].rearrange("p a n -> p (a n)"), ACT.Exp,
                                     bias=zst[:, 1:2], scale=SCALE,
                                     accum_out=zst[:, 2:3]).then_inc(zexp_done, 1)

            def z_hi(b):
                a.wait_ge(zrec_done, b + 1)
                if b >= 1:
                    a.wait_ge(z_out, 16 * b)
                nc.scalar.activation(zhl[:, 0, 0:S], ez[:, :], ACT.Copy,
                                     scale=zst[:, 3:4]).then_inc(zhi_done, 1)

            def evacuate(n, b, j):
                a.wait_ge(conv_done, n + 1)
                if j == 0 and not (isinstance(b, int) and b == 0):
                    a.wait_ge(aocur_done, b)
                dst = ao_acc[:, :, HG * HD * j:HG * HD * (j + 1)].rearrange("p i (h d) -> p h i d", h=HG)
                nc.scalar.activation(dst, ps_c.rearrange("p (h i d) -> p h i d", h=HG, d=HD),
                                     ACT.Copy).then_inc(aoevac_done, 1)

            a.wait_ge(eps_done, 1)
            nc.scalar.activation(warm[:, :], eps[:, :], ACT.Sqrt)
            std_of(0)
            turned_in(0)
            std_of(1)
            for t in range(NT):
                b, j = t // NJ, t % NJ
                if t + 1 < NT:
                    turned_in(t + 1)
                c = piece_at(t)
                if c is not None:
                    split_hi(c)
                    if c >= 1:
                        load_piece(a, c + 2)
                a.wait_ge(proj_done, t + 1)
                if j == 0 and b == 3:
                    a.wait_ge(v_out[0], 16)
                nc.scalar.activation(vb[V_SLOT[b]][:, 0, :, j, :],
                                     ps_p[t % NPS][:, NE + NH:NP].rearrange("p (h d) -> p h d", h=NH),
                                     ACT.Copy).then_inc(vhi_done, 1)
                if j == 2 and b >= 1:
                    z_exp(b - 1)
                if j == 5 and b >= 1:
                    z_hi(b - 1)
                if j == 0 and b + 2 < len(LN):
                    std_of(b + 2)
            a.wait_ge(xn_out, 16 * B)
            for c in range(LATE0, NPIECE):
                split_hi(c)
                if c + 2 < NPIECE:
                    load_piece(a, c + 2)
                if c == LATE0:
                    a.wait_ge(rsub_done, 1)
                    nc.scalar.activation(prob[:, :, :], prob[:, :, :], ACT.Exp).then_inc(route_exp, 1)
            for u in range(2 * NT // NB_E):
                a.wait_ge(oneh_done, u + 1)
                if u >= 2:
                    a.wait_ge(listmm_done, u - 1)
                k = NB_E * (u % 2)
                for i in range(0, NB_E, 2):
                    t = (NB_E * u + i) // 2
                    ins = nc.scalar.activation(oha[:, k + i:k + i + 2, 0, :], ohe[:, k + i:k + i + 2, :],
                                               ACT.Copy, scale=float(t + 1))
                ins.then_inc(tile_part, 1)
                if u == 0:
                    for b in range(B - 1):
                        a.wait_ge(v_out[b], 16)
                if u >= 4 and u % 2 == 0:
                    evacuate(u // 2 - 2, 0, u // 2 - 2)
            evacuate(LEAD - 1, 0, LEAD - 1)
            z_exp(B - 1)

            def x_hi(n):
                a.wait_ge(xtp_done, n + 1)
                nc.scalar.activation(xT[:, 0].rearrange("p k n -> p (k n)"), ps_x[:, :],
                                     ACT.Copy).then_inc(xhi_done, 1)

            def tile(n, b, j, conv, proj):
                for q in range(4):
                    a.wait_ge(g1_done, 4 * n + q + 1)
                    if not (isinstance(n, int) and n == 0 and q < 2):
                        a.wait_ge(glo_done, 4 * n + q - 1)
                    nc.scalar.activation(act[:, q % 2, :], ps_h[q][:, :], ACT.Gelu)
                    nc.scalar.activation(gh[:, 2 * q:2 * q + 2, :].rearrange("p c n -> p (c n)"), ps_h[q][:, :],
                                         ACT.Gelu).then_inc(gelu_done, 1)
                if not isinstance(n, int) or n + 1 < NTILE:
                    x_hi(n + 1)
                if proj:
                    turned(*proj)
                if conv:
                    evacuate(n + SH, *conv)
                if isinstance(n, int) and n == 0:
                    a.wait_ge(wo_in, 32)
                for m in range(2):
                    a.wait_ge(gate_done, n + 1)
                    a.wait_ge(g2_done, 2 * n + m + 1)
                    nc.scalar.activation(yt[:, m, :], ps_y[m][:, D:2 * D], ACT.Copy,
                                         scale=gate[:, m:m + 1]).then_inc(ylo_done, 1)

            def turned(b, j):
                a.wait_ge(aotp_done, NJ * b + j + 1)
                nc.scalar.activation(aoT[:, :, ::-1], ps_ot.rearrange("p (k n) -> p k n", k=KD),
                                     ACT.Copy).then_inc(aoT_done, 1)

            for j in range(LEAD, SH - 1):
                evacuate(j, 0, j)
            a.wait_ge(list_done, 1)
            x_hi(0)
            evacuate(SH - 1, 0, SH - 1)
            z_hi(B - 1)
            for_tiles(a, tile)

        @block.tensor
        def _(pe):
            def turn(t):
                pe.wait_ge(xn_done, t + 1)
                if t >= 2:
                    pe.wait_ge(xnT_done, t - 1)
                for k in range(KD):
                    ins = nc.tensor.transpose(ps_t[t % 2][:, k * P:(k + 1) * P],
                                              xw[:, t, k * P:(k + 1) * P], ident)
                ins.then_inc(tp_done, 1)

            def z_turn(b):
                pe.wait_ge(lg_done, NJ * (b + 1))
                if b >= 1:
                    pe.wait_ge(zexp_done, b)
                for j in range(NJ):
                    ins = nc.tensor.transpose(psz[0:NH, j // 4, (j % 4) * P:(j % 4 + 1) * P],
                                              lg[:, NJ * b + j, NE:NE + NH], ident)
                ins.then_inc(ztp_done, 1)

            pe.wait_ge(const_in, 32)
            pe.wait_ge(w_in, 48)
            turn(0)
            for t in range(NT):
                if t + 1 < NT:
                    turn(t + 1)
                pe.wait_ge(xnT_done, t + 1)
                if t >= NPS:
                    pe.wait_ge(post_done, t - NPS + 1)
                for k in range(KD):
                    ins = nc.tensor.matmul(ps_p[t % NPS][:, 0:NP], xnT[:, t % 2, k, :], wcat[:, k, :],
                                           start=(k == 0), stop=(k == KD - 1))
                ins.then_inc(proj_done, 1)
                if t % NJ == 0 and t > 0:
                    z_turn(t // NJ - 1)
            z_turn(B - 1)

            def convolve(n, b, j):
                pe.wait_ge(T_in[j % 2], 16 * (NJ // 2 * b + j // 2) + 16)
                if j == 0 and not (isinstance(b, int) and b == 0):
                    pe.wait_ge(v_in, 16 * b)
                if not (isinstance(n, int) and n == 0):
                    pe.wait_ge(aoevac_done, n)
                for h in range(HG):
                    for k in range(NJ):
                        for tl, vl in ((0, 0), (0, 1), (1, 0)):
                            v = vb[0][:, vl, HG * j + h, 0:NJ - k, :]
                            ins = nc.tensor.matmul(ps_c[:, h * P + k * HD:(h + 1) * P],
                                                   tz[:, j % 2, h, tl, (NJ - 1 - k) * P:(NJ - k) * P],
                                                   v.rearrange("p j d -> p (j d)"),
                                                   start=(k == 0 and tl + vl == 0),
                                                   stop=(k == NJ - 1 and tl == 1), skip_group_check=True)
                ins.then_inc(conv_done, 1)

            pe.wait_ge(mask_done, 1)
            pe.wait_ge(post_done, NT)
            prefix_t = prefix[:, :, :].rearrange("p e t -> p t e")
            nc.tensor.matmul(ps_cnt, cb[:, C_ONE:C_ONE + P], prefix[:, :, NT - 1],
                             start=True, stop=True).then_inc(cnt_done, 1)
            nc.tensor.matmul(ps_rank.rearrange("p (t e) -> p t e", e=NE), cb[:, C_ONE:C_ONE + P], prefix_t,
                             start=True, stop=False)
            nc.tensor.matmul(ps_rank, cb[:, C_UT:C_UT + P], maskb[:, :, :].rearrange("p t e -> p (t e)"),
                             start=False, stop=True).then_inc(cnt_done, 1)
            for u in range(2 * NT // NB_E):
                pe.wait_ge(tile_part, u + 1)
                pe.wait_ge(row_part, u + 1)
                pe.wait_ge(rows_done, u + 1)
                for i in range(NB_E):
                    s = NB_E * (u % 2) + i
                    ins = nc.tensor.matmul(ps_list, ohr[:, s, :], oha[:, s].rearrange("p v c -> p (v c)"),
                                           start=(u == 0 and i == 0), stop=(NB_E * u + i == 2 * NT - 1),
                                           skip_group_check=True)
                ins.then_inc(listmm_done, 1)
                if u >= 3 and u % 2 == 1:
                    convolve(u // 2 - 1, 0, u // 2 - 1)

            def x_turn(n, s, k):
                pe.wait_ge(g_in[s], 32 * k + 32)
                if not (isinstance(n, int) and n == 0):
                    pe.wait_ge(xlo_done, n)
                for k in range(KD):
                    for m in range(2):
                        ins = nc.tensor.transpose(ps_x[:, k * TS + m * P:k * TS + (m + 1) * P],
                                                  xs[:, s, m, k * P:(k + 1) * P], ident)
                ins.then_inc(xtp_done, 1)

            def turn_out(b, j):
                if j == 0:
                    pe.wait_ge(aocur_done, b + 1)
                else:
                    pe.wait_ge(at_done, NJ * b + j)
                for c in range(KD):
                    ins = nc.tensor.transpose(ps_ot[:, c * P:(c + 1) * P], ao[:, j, c * P:(c + 1) * P], ident)
                ins.then_inc(aotp_done, 1)

            def project_out(b, j):
                pe.wait_ge(aoT_done, NJ * b + j + 1)
                for c in range(KD):
                    ins = nc.tensor.matmul(ps_o, aoT[:, c, :], wo[:, c, :], start=(c == 0), stop=(c == KD - 1))
                ins.then_inc(wo_done, 1)

            def tile(n, b, j, conv, proj):
                e = pe.value_load(tei[0:1, bass.ds(n, 1)], min_val=0, max_val=NE - 1)
                pe.wait_ge(xlo_done, n + 1)
                for q in range(4):
                    if q == 3:
                        pe.wait_ge(gelu_done, 4 * n + 1)
                    elif not (isinstance(n, int) and n == 0):
                        pe.wait_ge(gelu_done, 4 * n if q == 0 else 4 * n + q - 3)
                    for c in (2 * q, 2 * q + 1):
                        o = ps_h[q][:, (c % 2) * TS:(c % 2 + 1) * TS]
                        for k in range(KD):
                            for wl, xl in ((0, 0), (0, 1), (1, 0)):
                                ins = nc.tensor.matmul(o, w1s[:, e, wl, k, c * P:(c + 1) * P], xT[:, xl, k, :],
                                                       start=(k == 0 and wl + xl == 0),
                                                       stop=(k == KD - 1 and wl == 1))
                    ins.then_inc(g1_done, 1)
                if not isinstance(n, int) or n + 1 < NTILE:
                    x_turn(n + 1, (j + 1) % 2, (NJ // 2) * b + (j + 1) // 2)
                if proj:
                    turn_out(*proj)
                if conv:
                    convolve(n + SH, *conv)
                if isinstance(n, int) and n == 0:
                    pe.wait_ge(wo_in, 32)
                if proj and conv:
                    project_out(*proj)
                for m in range(2):
                    if not (isinstance(n, int) and n == 0):
                        pe.wait_ge(y_done, 2 * n + m - 1)
                    for c in range(KH):
                        if m == 0 and c % 2 == 0:
                            pe.wait_ge(glo_done, 4 * n + c // 2 + 1)
                        nc.tensor.matmul(ps_y[m], gh[:, c, m * P:(m + 1) * P], w2s[:, e, c, :],
                                         start=(c == 0), stop=False, skip_group_check=True)
                        ins = nc.tensor.matmul(ps_y[m][:, 0:D], gl[:, c, m * P:(m + 1) * P], w2s[:, e, c, 0:D],
                                               start=False, stop=(c == KH - 1), skip_group_check=True)
                    ins.then_inc(g2_done, 1)
                    if m == 0 and proj and not conv:
                        project_out(*proj)

            pe.wait_ge(wlo_done, NPIECE)
            for j in range(LEAD, SH - 1):
                convolve(j, 0, j)
            pe.wait_ge(list_done, 1)
            pe.wait_ge(zexp_done, B)
            x_turn(0, 0, 0)
            convolve(SH - 1, 0, SH - 1)
            pe.wait_ge(tiles_done, 1)
            for_tiles(pe, tile)

        @block.vector
        def _(v):
            def stats(t):
                if t % NJ == 0:
                    v.wait_ge(x_in[t // NJ], 16)
                elif t == NJ // 2:
                    v.wait_ge(x_in[4], 16)
                nc.vector.bn_stats(st[:, t % NJ, :], xw[:, t, :]).then_inc(stats_done, 1)
                v.wait_ge(stats_done, t + 1)
                nc.vector.bn_aggr(mv[:, t, :], st[:, t % NJ, :]).then_inc(aggr_done, 1)

            def norm(t):
                for g, (lo, hi) in enumerate(LN):
                    if t == lo:
                        v.wait_ge(std_done, g + 1)
                        nc.vector.reciprocal(rstd[:, lo:hi], std[:, lo:hi]).then_inc(rstd_done, 1)
                        v.wait_ge(rstd_done, g + 1)
                nc.vector.tensor_scalar(xw[:, t, :], xw[:, t, :], mv[:, t, 0:1], rstd[:, t:t + 1],
                                        ALU.subtract, ALU.mult).then_inc(xn_done, 1)

            def post(t):
                slot = vb[V_SLOT[t // NJ]]
                v.wait_ge(vhi_done, t + 1)
                nc.vector.tensor_copy(lg[:, t, :], ps_p[t % NPS][:, 0:NE + NH]).then_inc(lg_done, 1)
                nc.vector.tensor_tensor(slot[:, 1, :, t % NJ, :],
                                        ps_p[t % NPS][:, NE + NH:NP].rearrange("p (h d) -> p h d", h=NH),
                                        slot[:, 0, :, t % NJ, :], ALU.subtract).then_inc(post_done, 1)

            def z_max(b):
                v.wait_ge(ztp_done, b + 1)
                nc.vector.tensor_reduce(zst[:, 0:1], psz[0:NH, :, :].rearrange("p a n -> p (a n)"), AX.X,
                                        ALU.max).then_inc(zmax_done, 1)
                v.wait_ge(zmax_done, b + 1)
                nc.vector.tensor_scalar(zst[:, 1:2], zst[:, 0:1], -SCALE, None, ALU.mult).then_inc(zneg_done, 1)

            def z_scale(b):
                v.wait_ge(zexp_done, b + 1)
                nc.vector.reciprocal(zst[:, 3:4], zst[:, 2:3]).then_inc(zrec_done, 1)

            def z_low(b):
                v.wait_ge(zhi_done, b + 1)
                if b == 0:
                    v.wait_ge(zpad_done, 1)
                nc.vector.scalar_tensor_tensor(zhl[:, 1, 0:S], ez[:, :], zst[:, 3:4], zhl[:, 0, 0:S],
                                               ALU.mult, ALU.subtract).then_inc(zsplit_done, 1)

            nc.vector.memset(eps[:, :], EPS).then_inc(eps_done, 1)
            nc.vector.memset(first[:, :, :], 1.0).then_inc(first_done, 1)
            v.wait_ge(first_done, 1)
            nc.vector.memset(first[:, :, 0:1], 0.0).then_inc(first_done, 1)
            for lo, hi in LN[0:2]:
                for t in range(lo, hi):
                    stats(t)
                for t in range(lo, hi):
                    norm(t)
            for t in range(NJ, 2 * NJ):
                stats(t)
            for t in range(NT):
                b, j = t // NJ, t % NJ
                if b + 1 < B:
                    norm(t + NJ)
                post(t)
                if b + 2 < B:
                    stats(t + 2 * NJ)
                if b >= 1:
                    if j == 1:
                        z_max(b - 1)
                    if j == 4:
                        z_scale(b - 1)
                    if j == 6:
                        z_low(b - 1)

            done = [0]

            def step(ins):
                done[0] += 1
                ins.then_inc(route, 1)
                v.wait_ge(route, done[0])

            def wide(col):
                return col.unsqueeze(2).to_broadcast([P, NT, NE])

            v.wait_ge(lg_done, NT)
            c = [c32[:, i, :] for i in range(4)]
            step(nc.vector.tensor_reduce(c[0], lg[:, :, 0:NE], AX.X, ALU.max))
            nc.vector.tensor_tensor(prob[:, :, :], lg[:, :, 0:NE], wide(c[0]), ALU.subtract).then_inc(rsub_done, 1)
            v.wait_ge(route_exp, 1)
            step(nc.vector.tensor_reduce(c[1], prob[:, :, :], AX.X, ALU.add))
            step(nc.vector.reciprocal(c[2], c[1]))
            step(nc.vector.tensor_tensor(prob[:, :, :], prob[:, :, :], wide(c[2]), ALU.mult))
            ew = cf[:, C_EW:C_EW + NE].unsqueeze(1).to_broadcast([P, NT, NE])
            left = prob
            for oh in (oh1, oh2):
                step(nc.vector.tensor_reduce(c[0], left[:, :, :], AX.X, ALU.max))
                step(nc.vector.tensor_tensor(oh[:, :, :], left[:, :, :], wide(c[0]), ALU.is_equal))
                step(nc.vector.tensor_tensor(oh[:, :, :], oh[:, :, :], ew, ALU.mult))
                step(nc.vector.tensor_reduce(c[1], oh[:, :, :], AX.X, ALU.max))
                step(nc.vector.tensor_tensor(oh[:, :, :], oh[:, :, :], wide(c[1]), ALU.is_equal))
                if oh is oh1:
                    step(nc.vector.scalar_tensor_tensor(t8[:, :, :], oh1[:, :, :], -2.0, prob[:, :, :],
                                                        ALU.mult, ALU.add))
                    left = t8
            both = rank[:, :, :].rearrange("p t e -> p (t e)")
            both_te = both.rearrange("p (e t) -> p t e", e=NE)
            step(nc.vector.tensor_tensor(both_te, oh1[:, :, :], oh2[:, :, :], ALU.add))
            v.wait_ge(first_done, 2)
            step(nc.vector.tensor_tensor_scan(prefix[:, :, :].rearrange("p e t -> p (e t)"),
                                              first[:, :, :].rearrange("p e t -> p (e t)"),
                                              both, 0.0, ALU.mult, ALU.add))
            nc.vector.tensor_copy(maskb[:, :, :], both_te).then_inc(mask_done, 1)
            nc.vector.tensor_tensor(t8[:, :, :], both_te, prob[:, :, :], ALU.mult).then_inc(gates_done, 1)

            v.wait_ge(cnt_done, 1)
            e = [e8[:, i, :] for i in range(6)]
            step(nc.vector.tensor_scalar(e8i[:, 0, :], ps_cnt, float(TS - 1), None, ALU.add))
            step(nc.vector.tensor_scalar(e8i[:, 1, :], e8i[:, 0, :], 8, None, ALU.arith_shift_right))
            step(nc.vector.tensor_copy(e[0], e8i[:, 1, :]))
            step(nc.vector.memset(e[1], 1.0))
            step(nc.vector.tensor_tensor_scan(e[2], e[1], e[0], 0.0, ALU.mult, ALU.add))
            step(nc.vector.tensor_tensor(e[3], e[2], e[0], ALU.subtract))
            step(nc.vector.tensor_scalar(e[4], e[3], float(TS), None, ALU.mult))
            v.wait_ge(cnt_done, 2)
            step(nc.vector.tensor_tensor(rank[:, :, :], ps_rank.rearrange("p (t e) -> p t e", e=NE),
                                         e[4].unsqueeze(1).to_broadcast([P, NT, NE]), ALU.add))
            for i, oh in enumerate((oh1, oh2)):
                step(nc.vector.tensor_tensor(oh[:, :, :], oh[:, :, :], rank[:, :, :], ALU.mult))
                step(nc.vector.tensor_reduce(posf[:, :, i], oh[:, :, :], AX.X, ALU.add))
            pf, pi = (z[:, :, :].rearrange("p t a -> p (t a)") for z in (posf, posi))
            step(nc.vector.tensor_copy(pi, pf))
            step(nc.vector.tensor_scalar(pi, pi, 7, None, ALU.arith_shift_right))
            step(nc.vector.tensor_copy(colA[:, :], pi))
            step(nc.vector.scalar_tensor_tensor(colR[:, :], colA[:, :], -float(P), pf, ALU.mult, ALU.add))

            def one_hots(u):
                if u >= 2:
                    v.wait_ge(tile_part, u - 1)
                    v.wait_ge(row_part, u - 1)
                k, s = NB_E * u, NB_E * (u % 2)
                nc.vector.tensor_tensor(ohe[:, s:s + NB_E, :],
                                        cb[:, C_IA:C_IA + NCOL].unsqueeze(1).to_broadcast([P, NB_E, NCOL]),
                                        colA[:, k:k + NB_E].unsqueeze(2).to_broadcast([P, NB_E, NCOL]),
                                        ALU.is_equal).then_inc(oneh_done, 1)
                if u >= 2:
                    v.wait_ge(listmm_done, u - 1)
                nc.vector.tensor_tensor(ohr[:, s:s + NB_E, :],
                                        cb[:, C_IR:C_IR + P].unsqueeze(1).to_broadcast([P, NB_E, P]),
                                        colR[:, k:k + NB_E].unsqueeze(2).to_broadcast([P, NB_E, P]),
                                        ALU.is_equal).then_inc(rows_done, 1)

            for u in range(2 * NT // NB_E):
                one_hots(u)
            v.wait_ge(listmm_done, 2 * NT // NB_E)
            step(nc.vector.tensor_copy(idf[:, :, :].rearrange("p v c -> p (v c)"), ps_list))
            step(nc.vector.scalar_tensor_tensor(idf[:, 1, :], idf[:, 0, :], float(P), idf[:, 1, :],
                                                ALU.mult, ALU.add))
            step(nc.vector.tensor_scalar(idf[:, 0, :], idf[:, 0, :], 0.0, None, ALU.is_equal))
            step(nc.vector.tensor_tensor(idf[:, 0, :], idf[:, 0, :], cf[:, C_PAD:C_PAD + NCOL], ALU.mult))
            step(nc.vector.tensor_tensor(idf[:, 1, :], idf[:, 1, :], idf[:, 0, :], ALU.add))
            nc.vector.tensor_scalar(idt[:, :], idf[:, 1, :], -float(P), None, ALU.add).then_inc(list_done, 1)
            step(nc.vector.memset(ge9[:, :, 0:1], 1.0))
            step(nc.vector.memset(ge9[:, :, NE:NE + 1], 0.0))
            step(nc.vector.tensor_tensor(
                ge9[:, :, 1:NE], cf[:, C_S:C_S + NTILE].unsqueeze(2).to_broadcast([P, NTILE, NE - 1]),
                e8[:, 2, 0:NE - 1].unsqueeze(1).to_broadcast([P, NTILE, NE - 1]), ALU.is_ge))
            step(nc.vector.tensor_tensor(teoh[:, :, :], ge9[:, :, 0:NE], ge9[:, :, 1:NE + 1], ALU.subtract))
            step(nc.vector.tensor_reduce(tef[:, :], ge9[:, :, 1:NE], AX.X, ALU.add))
            step(nc.vector.tensor_copy(tei[:, 0:NTILE], tef[:, :]))
            nc.vector.tensor_copy(tei[:, NTILE:NTILE + 1], e8[:, 2, NE - 1:NE]).then_inc(tiles_done, 1)
            z_max(B - 1)

            def x_lo(n):
                v.wait_ge(xhi_done, n + 1)
                nc.vector.tensor_tensor(xT[:, 1].rearrange("p k n -> p (k n)"), ps_x[:, :],
                                        xT[:, 0].rearrange("p k n -> p (k n)"), ALU.subtract).then_inc(xlo_done, 1)

            def gates(n, s, k):
                v.wait_ge(g_in[s], 32 * k + 32)
                nc.vector.tensor_tensor(g8[:, :, :], xs[:, s, :, D:ROW],
                                        teoh[:, bass.ds(n, 1), :].to_broadcast([P, 2, NE]),
                                        ALU.mult).then_inc(g8_done, 1)
                v.wait_ge(g8_done, n + 1)
                nc.vector.tensor_reduce(gate[:, :], g8[:, :, :], AX.X, ALU.add).then_inc(gate_done, 1)

            def rows(b, j):
                v.wait_ge(wo_done, NJ * b + j + 1)
                nc.vector.tensor_tensor(at[:, j % 4, :], ps_o, bo[:, :], ALU.add).then_inc(at_done, 1)

            def tile(n, b, j, conv, proj):
                if proj and proj[1] == 0:
                    v.wait_ge(aoevac_done, n + SH)
                    nc.vector.tensor_copy(ao[:, :, :], ao_acc[:, :, :]).then_inc(aocur_done, 1)
                for q in range(4):
                    v.wait_ge(gelu_done, 4 * n + q + 1)
                    nc.vector.tensor_tensor(gl[:, 2 * q:2 * q + 2, :].rearrange("p c n -> p (c n)"),
                                            act[:, q % 2, :],
                                            gh[:, 2 * q:2 * q + 2, :].rearrange("p c n -> p (c n)"),
                                            ALU.subtract).then_inc(glo_done, 1)
                more = not isinstance(n, int) or n + 1 < NTILE
                if more:
                    x_lo(n + 1)
                if proj and conv:
                    rows(*proj)
                if isinstance(n, int) and n == 0:
                    v.wait_ge(wo_in, 32)
                for m in range(2):
                    v.wait_ge(ylo_done, 2 * n + m + 1)
                    if not (isinstance(n, int) and n == 0):
                        static = isinstance(n, int)
                        at_end = acc_before(n - 1, b, j - 1) + 1 if j or static else acc_before(n, b, 0) - 2
                        v.wait_ge(acc_out, 16 * (at_end + m))
                    nc.vector.scalar_tensor_tensor(y[:, m, :], ps_y[m][:, 0:D], gate[:, m:m + 1], yt[:, m, :],
                                                   ALU.mult, ALU.add).then_inc(y_done, 1)
                    if m == 0 and proj and not conv:
                        rows(*proj)
                if more:
                    gates(n + 1, (j + 1) % 2, (NJ // 2) * b + (j + 1) // 2)

            x_lo(0)
            gates(0, 0, 0)
            z_scale(B - 1)
            z_low(B - 1)
            for_tiles(v, tile)


def kernel(**inputs):
    import numpy as np
    import ml_dtypes
    import concourse.bacc as bacc
    from concourse import mybir as mb
    from concourse.bass_utils import run_bass_kernel_spmd as run

    cf = np.zeros((P, C_F), np.float32)
    cf[:, C_ID:C_ID + P] = np.eye(P)
    cf[:, C_P] = np.arange(P)
    cf[:, C_EW:C_EW + NE] = NE - np.arange(NE)
    cf[:, C_S:C_S + NTILE] = np.arange(NTILE)
    cf[:, C_PAD:C_PAD + NCOL] = P + TOK + (np.arange(NCOL) % 2)[None, :] * P + np.arange(P)[:, None]
    cb = np.zeros((P, C_B), np.float32)
    cb[:, C_UT:C_UT + P] = np.triu(np.ones((P, P)), 1) - 1
    cb[:, C_ONE:C_ONE + P] = 1
    cb[:, C_IR:C_IR + P] = np.arange(P)
    cb[:, C_IA:C_IA + NCOL] = np.arange(NCOL)
    cb = cb.astype(ml_dtypes.bfloat16)

    def laid(a, *order):
        a = np.asarray(a)
        return np.ascontiguousarray(a.transpose(order) if order else a)

    arrays = {
        "x": laid(inputs["L0_attn_x"]).reshape(TOK, D),
        "routerT": laid(inputs["L0_ffn_router_w"], 1, 0),
        "waT": laid(inputs["L0_attn_W_A"], 1, 0),
        "wvT": laid(inputs["L0_attn_W_V"], 1, 0),
        "woT": laid(inputs["L0_attn_W_O"], 1, 0),
        "b_o": laid(inputs["L0_attn_b_O"]),
        "w1T": laid(inputs["L0_ffn_w1"], 0, 2, 1),
        "w2T": laid(inputs["L0_ffn_w2"], 0, 2, 1),
        "const_f": cf,
        "const_b": cb,
        "zeros": np.zeros((PADROWS, ROW), np.float32),
    }
    nc = bacc.Bacc("TRN2", target_bir_lowering=False, num_devices=1)
    args = [nc.dram_tensor(n, a.shape, mb.dt.from_np(a.dtype), kind="ExternalInput").ap() for n, a in arrays.items()]
    args.append(nc.dram_tensor("out", (TOK + PADROWS, D), F32, kind="ExternalOutput").ap())
    build(nc, *args)
    r = run(nc, [arrays], core_ids=[0])
    return r.results[0]["out"][0:TOK].reshape(B, S, D)
```
